# Optimizing a Trainium2 kernel written in Bass

```python
import numpy as np
import jax
import jax.numpy as jnp

def _softmax(x, axis=-1):
    return jax.nn.softmax(x, axis=axis)

def _gelu(x):
    return jax.nn.gelu(x, approximate=True)

def _silu(x):
    return jax.nn.silu(x)

def _sigmoid(x):
    return jax.nn.sigmoid(x)

def _layernorm(x, axis=-1, eps=1e-05):
    m = jnp.mean(x, axis=axis, keepdims=True)
    v = jnp.var(x, axis=axis, keepdims=True)
    return (x - m) / jnp.sqrt(v + eps)

def _scatter_add(tgt, idx, src, axis=0):
    return tgt.at[idx].add(src)

def _segment_sum(src, seg, n):
    return jax.ops.segment_sum(src, seg, n)
kernel_name = 'mk_xattn_ffn_d1_seqx_r4_8cfda9'

def setup_inputs(seed: int=0):
    np.random.seed(seed)
    _w = jnp.asarray

    def _rec_inputs():
        import jax
        import jax.numpy as jnp
        _rk = jax.random.key(seed)
        x = 0.0002417 + 0.9998 * jax.random.normal(jax.random.fold_in(_rk, 1), (32, 112, 256), jnp.float32)
        _lenS = 112 - jax.random.randint(jax.random.fold_in(_rk, 7), (32,), 0, max(1, 112 // 4) + 1, jnp.int32)
        _lenS2 = 375 - jax.random.randint(jax.random.fold_in(_rk, 8), (32,), 0, max(1, 375 // 4) + 1, jnp.int32)
        _ctx_1024P = jax.random.normal(jax.random.fold_in(_rk, 11), (32, 16, 256), jnp.float32)
        _ctx_1024c = jax.random.dirichlet(jax.random.fold_in(_rk, 511), 0.3 * jnp.ones((16,), jnp.float32), (32, 375))
        _ctx_1024t = jnp.einsum('bsk,bkd->bsd', _ctx_1024c, _ctx_1024P)
        _ctx_1024t = _ctx_1024t * jax.lax.rsqrt(jnp.mean(jnp.square(_ctx_1024t)) + 1e-12) * 0.953939
        ctx_1024 = 7.22013e-05 + 1.00017 * (_ctx_1024t + 0.3 * jax.random.normal(jax.random.fold_in(_rk, 611), (32, 375, 256), jnp.float32))
        _validS = jnp.arange(112)[None, :] < _lenS[:, None]
        _validS2 = jnp.arange(375)[None, :] < _lenS2[:, None]
        _causal = jnp.tril(jnp.ones((112, 112), dtype=bool))
        mask_1x1xSxS2_fk1 = jnp.where(jnp.broadcast_to(_validS2[0:1, None, None, :], (1, 1, 112, 375)), 1.0, 0.0).astype(jnp.float32)
        return (x, ctx_1024, mask_1x1xSxS2_fk1)
    x, ctx_1024, mask_1x1xSxS2_fk1 = _rec_inputs()

    def _L0_xattn_setup():
        import jax, jax.numpy as jnp
        import numpy as np
        D_MODEL = 256
        NUM_HEADS = 16
        DEPTH = D_MODEL // NUM_HEADS
        BATCH = 4
        SEQ = 512
        NEG_BIG = -1000000000.0

        def _split_heads(x, b, s):
            return x.reshape(b, s, NUM_HEADS, DEPTH).transpose(0, 2, 1, 3)
        key = jax.random.key(seed)
        ks = jax.random.split(key, 12)
        f = lambda k, shape, scale=1.0: jax.random.normal(k, shape, dtype=jnp.float32) * scale
        inv = 1.0 / np.sqrt(D_MODEL)
        mask = jnp.triu(jnp.ones((SEQ, SEQ), dtype=jnp.float32), k=1)[None, None, :, :]
        return {'v': f(ks[0], (BATCH, SEQ, D_MODEL)), 'k': f(ks[1], (BATCH, SEQ, D_MODEL)), 'q': f(ks[2], (BATCH, SEQ, D_MODEL)), 'mask': mask, 'wq_w': f(ks[3], (D_MODEL, D_MODEL), inv), 'wq_b': jnp.zeros((D_MODEL,), jnp.float32), 'wk_w': f(ks[4], (D_MODEL, D_MODEL), inv), 'wk_b': jnp.zeros((D_MODEL,), jnp.float32), 'wv_w': f(ks[5], (D_MODEL, D_MODEL), inv), 'wv_b': jnp.zeros((D_MODEL,), jnp.float32), 'wo_w': f(ks[6], (D_MODEL, D_MODEL), inv), 'wo_b': jnp.zeros((D_MODEL,), jnp.float32)}
    _L0_xattn_all = _L0_xattn_setup()
    _L0_xattn_in = {k: v for k, v in _L0_xattn_all.items() if k in ('wq_w', 'wq_b', 'wk_w', 'wk_b', 'wv_w', 'wv_b', 'wo_w', 'wo_b')}
    del _L0_xattn_all

    def _L0_ffn_setup():
        import jax, jax.numpy as jnp
        import numpy as np
        B, T, D, F, E = (2, 256, 256, 1024, 8)
        EPS = 1e-06
        key = jax.random.key(seed)
        k = jax.random.split(key, 5)
        scale = 0.02
        return {'x': jax.random.normal(k[0], (B, T, D), dtype=jnp.float32), 'rms_w': jnp.ones((D,), dtype=jnp.float32), 'gate_w': jax.random.normal(k[1], (E, D), dtype=jnp.float32) * scale, 'W1': jax.random.normal(k[2], (E, D, F), dtype=jnp.float32) * scale, 'b1': jnp.zeros((E, F), dtype=jnp.float32), 'W2': jax.random.normal(k[3], (E, F, D), dtype=jnp.float32) * scale, 'b2': jnp.zeros((E, D), dtype=jnp.float32)}
    _L0_ffn_all = _L0_ffn_setup()
    _L0_ffn_in = {k: v for k, v in _L0_ffn_all.items() if k in ('rms_w', 'gate_w', 'W1', 'b1', 'W2', 'b2')}
    del _L0_ffn_all
    return {'x': x, 'ctx_1024': ctx_1024, 'mask_1x1xSxS2_fk1': mask_1x1xSxS2_fk1, 'L0_xattn_wq_w': _L0_xattn_in['wq_w'], 'L0_xattn_wq_b': _L0_xattn_in['wq_b'], 'L0_xattn_wk_w': _L0_xattn_in['wk_w'], 'L0_xattn_wk_b': _L0_xattn_in['wk_b'], 'L0_xattn_wv_w': _L0_xattn_in['wv_w'], 'L0_xattn_wv_b': _L0_xattn_in['wv_b'], 'L0_xattn_wo_w': _L0_xattn_in['wo_w'], 'L0_xattn_wo_b': _L0_xattn_in['wo_b'], 'L0_ffn_rms_w': _L0_ffn_in['rms_w'], 'L0_ffn_gate_w': _L0_ffn_in['gate_w'], 'L0_ffn_W1': _L0_ffn_in['W1'], 'L0_ffn_b1': _L0_ffn_in['b1'], 'L0_ffn_W2': _L0_ffn_in['W2'], 'L0_ffn_b2': _L0_ffn_in['b2']}

def reference(x, ctx_1024, mask_1x1xSxS2_fk1, L0_xattn_wq_w, L0_xattn_wq_b, L0_xattn_wk_w, L0_xattn_wk_b, L0_xattn_wv_w, L0_xattn_wv_b, L0_xattn_wo_w, L0_xattn_wo_b, L0_ffn_rms_w, L0_ffn_gate_w, L0_ffn_W1, L0_ffn_b1, L0_ffn_W2, L0_ffn_b2):
    import jax
    import jax.numpy as jnp

    def _L0_xattn_ref(v, k, q, mask, wq_w, wq_b, wk_w, wk_b, wv_w, wv_b, wo_w, wo_b):
        import jax, jax.numpy as jnp
        import numpy as np
        D_MODEL = 256
        NUM_HEADS = 16
        DEPTH = D_MODEL // NUM_HEADS
        BATCH = 4
        SEQ = 512
        NEG_BIG = -1000000000.0

        def _split_heads(x, b, s):
            return x.reshape(b, s, NUM_HEADS, DEPTH).transpose(0, 2, 1, 3)
        b, sq, _ = q.shape
        sk = k.shape[1]
        qh = _split_heads(q @ wq_w + wq_b, b, sq)
        kh = _split_heads(k @ wk_w + wk_b, b, sk)
        vh = _split_heads(v @ wv_w + wv_b, b, sk)
        logits = jnp.einsum('bhqd,bhkd->bhqk', qh, kh) / jnp.sqrt(jnp.float32(DEPTH))
        logits = logits + mask * NEG_BIG
        attn = jax.nn.softmax(logits, axis=-1)
        out = jnp.einsum('bhqk,bhkd->bhqd', attn, vh)
        out = out.transpose(0, 2, 1, 3).reshape(b, sq, D_MODEL)
        return out @ wo_w + wo_b

    def _L0_ffn_ref(x, rms_w, gate_w, W1, b1, W2, b2):
        import jax, jax.numpy as jnp
        import numpy as np
        B, T, D, F, E = (2, 256, 256, 1024, 8)
        EPS = 1e-06
        ms = jnp.mean(x * x, axis=-1, keepdims=True)
        xn = x * jax.lax.rsqrt(ms + EPS) * rms_w
        logits = jnp.einsum('btd,ed->bte', xn, gate_w)
        scores = jax.nn.softmax(logits, axis=-1)
        top1_idx = jnp.argmax(scores, axis=-1)
        top1_score = jnp.max(scores, axis=-1)
        out = jnp.zeros_like(xn)
        for e in range(E):
            h = jax.nn.silu(jnp.einsum('btd,df->btf', xn, W1[e]) + b1[e])
            ye = jnp.einsum('btf,fd->btd', h, W2[e]) + b2[e]
            out = jnp.where((top1_idx == e)[..., None], ye, out)
        return out * top1_score[..., None]
    x = x + _L0_xattn_ref(ctx_1024, ctx_1024, _layernorm(x, axis=-1), mask_1x1xSxS2_fk1, L0_xattn_wq_w, L0_xattn_wq_b, L0_xattn_wk_w, L0_xattn_wk_b, L0_xattn_wv_w, L0_xattn_wv_b, L0_xattn_wo_w, L0_xattn_wo_b)
    x = x + _L0_ffn_ref(_layernorm(x, axis=-1), L0_ffn_rms_w, L0_ffn_gate_w, L0_ffn_W1, L0_ffn_b1, L0_ffn_W2, L0_ffn_b2)
    return x

_drawn_inputs = setup_inputs


def setup_inputs(seed=0):
    import zlib

    import numpy as np

    out = dict(_drawn_inputs(seed))
    spreads = {'L0_xattn_wq_b': (0.0, 0.345),
     'L0_xattn_wk_b': (0.0, 0.8),
     'L0_xattn_wv_b': (0.0, 0.1),
     'L0_xattn_wo_b': (0.0, 0.1),
     'L0_ffn_rms_w': (1.0, 0.6),
     'L0_ffn_b1': (0.0, 0.8),
     'L0_ffn_b2': (0.0, 0.454)}
    factors = {'L0_ffn_W1': 2.927, 'L0_ffn_W2': 2.767}
    for name, (base, spread) in spreads.items():
        noise = np.random.default_rng([zlib.crc32(name.encode()), seed]).standard_normal(out[name].shape)
        drawn = base * np.exp(spread * noise) if base else spread * noise
        out[name] = jnp.asarray(drawn.astype(out[name].dtype))
    for name, factor in factors.items():
        out[name] = (out[name] * factor).astype(out[name].dtype)
    return out
```

```python
from contextlib import ExitStack

import concourse.bass as bass
from concourse import mybir

ALU = mybir.AluOpType
ACT = mybir.ActivationFunctionType
F32 = mybir.dt.float32
F16 = mybir.dt.float16
I32 = mybir.dt.int32
U32 = mybir.dt.uint32
AX_X = mybir.AxisListType.X

P = 128
B, T, D = 32, 112, 256
S, CHUNKS = 375, 3
CK = S // CHUNKS
H = 16
DH = D // H
DT = D // P
HPT = H // DT
VW = DH + 1
NEG_BIG = -1e9
EXPERTS, F = 8, 1024
FT = F // P
FFN_TILES = (B * T + EXPERTS * (P - 1)) // P
GROUPS = ((0, 0), (0, 1), (1, 0), (1, 1))
PAIRS = P // (2 * DH)
SCALE_K, SCALE_Q = 64.0, 64.0
SCALE_SCORES = SCALE_K * SCALE_Q
LN_EPS, RMS_EPS = 1e-5, 1e-6
HEAD_LAG_T, HEAD_LAG_COPY = 3, 4
PEELED_FIRST, UNROLL = 4, 2


class Step:

    def __init__(self, base, i=0, in_loop=False):
        self.base, self.i, self.in_loop = base, i, in_loop

    def batch(self, lag):
        return self.i * UNROLL + (self.base - lag) if self.in_loop else self.base - lag

    def exists(self, lag):
        return self.in_loop or 0 <= self.base - lag < B

    def parity(self, lag):
        return (self.base - lag) % 2

    def half(self, lag):
        return self.i + (self.base - lag) // 2 if self.in_loop else (self.base - lag) // 2


def run_steps(eng, body):
    for s in range(-1, PEELED_FIRST):
        body(Step(s))
    with eng.Fori(0, (B - 2 - PEELED_FIRST) // UNROLL) as i:
        for k in range(UNROLL):
            body(Step(PEELED_FIRST + k, i, True))
    for s in range(B - 2, B + 2):
        body(Step(s))


def wait_count(eng, sem, value):
    if not isinstance(value, int) or value > 0:
        eng.wait_ge(sem, value)


def wait_apart(eng, sem, value, passed):
    eng.wait_ge(sem, value)
    eng.sem_inc(passed, 1)


def build(nc, x, ctx, mask, wq, bq, wk, bk, wv, bv, wo, bo, rms_w, gate_w, w1, b1, w2, b2, out):
    sorted_rows = nc.dram_tensor("sorted_rows", [FFN_TILES * P, D], F32).ap()
    sorted_y = nc.dram_tensor("sorted_y", [FFN_TILES * P, D], F32).ap()
    x1_rows = nc.dram_tensor("x1_rows", [B, T, D], F32).ap()
    q_spill = [nc.dram_tensor(f"q_spill{i}", [2, P, DT * 2 * T], F16).ap() for i in range(2)]
    k_spill = [nc.dram_tensor(f"k_spill{i}", [2, P, DT * S], F16).ap() for i in range(2)]

    with ExitStack() as stack:
        def sb(name, shape, dt=F32):
            return stack.enter_context(nc.sbuf_tensor(name, shape, dt))

        def sem(name):
            return stack.enter_context(nc.semaphore(name))

        arena_a = sb("arena_a", [P, EXPERTS * FT * D])
        arena_b = sb("arena_b", [P, 9216])
        used = {"a": 0, "b": 0}

        def carve(which, parts, *shape):
            arena = arena_a if which == "a" else arena_b
            n = 1
            for d in shape:
                n *= d
            at = used[which]
            used[which] += n + n % 2
            assert used[which] <= arena.shape[1]
            flat = arena[0:parts, at:at + n]
            if len(shape) == 1:
                return flat
            names = "abcd"[:len(shape)]
            return flat.rearrange(f"p ({' '.join(names)}) -> p {' '.join(names)}",
                                  **{k: v for k, v in zip(names, shape)})

        ident = sb("ident", [P, P])
        w1_sb = sb("w1_sb", [P, EXPERTS, DT, F])
        xr_all = sb("xr_all", [T, B, D])
        gate_logits = sb("gate_logits", [T, B, EXPERTS])
        score = sb("score", [T, B])
        slot_of = sb("slot_of", [T, B], U32)
        tile_expert = sb("tile_expert", [1, FFN_TILES + 1], I32)

        wq_sb = carve("a", P, DT, D)
        wk_sb = carve("a", P, DT, D)
        wv_sb = carve("a", P, DT, D)
        wo_sb = carve("a", P, DT, D)
        gw_sb = carve("a", P, DT, EXPERTS)
        gw_rows = carve("a", EXPERTS, D)
        bq_sb = carve("a", P, DT)
        bk_sb = carve("a", P, DT)
        bv_cols = carve("a", P, DT)
        bv_rep = carve("a", P, DT, T)
        bvo = carve("a", T, D)
        rmsw = carve("a", T, D)
        mask_bias = carve("a", T, S)
        pair_rows = carve("a", P, 2)
        eps_ln = carve("a", T, 1)
        eps_rms = carve("a", T, 1)
        minus_half = carve("a", T, 1)
        x_in = [carve("a", T, D) for _ in range(2)]
        x_res = [carve("a", T, D) for _ in range(2)]
        xn = carve("a", T, D)
        xnT = carve("a", P, DT, T)
        q1 = carve("a", P, DT, T)
        q_masked = carve("a", P, DT, 2, T)
        q_parts = carve("a", P, 2 * DT * T).bitcast(F16).rearrange("p (s j a t) -> p s j a t", s=2, j=DT, a=2)
        k_parts = carve("a", P, DT * S).bitcast(F16).rearrange("p (s j k) -> p s j k", s=2, j=DT)
        q_stack = [carve("a", P, PAIRS * DT * T).bitcast(F16).rearrange("p (r j a t) -> p r j a t", r=PAIRS, j=DT, a=2)
                   for _ in range(2)]
        ctx_in = [carve("b", CK, CHUNKS, D) for _ in range(2)]
        ctxT = carve("b", P, DT, S)
        k_stack_words = [carve("a", P, PAIRS * DT * S // 2) for _ in range(2)]
        k_stack = [words.bitcast(F16).rearrange("p (r j k) -> p r j k", r=PAIRS, j=DT) for words in k_stack_words]
        wq_in, wk_in = [words[:, 0:DT * D].rearrange("p (t d) -> p t d", t=DT) for words in k_stack_words]
        v_aug = [carve("b", CK, CHUNKS, H, VW) for _ in range(2)]
        probs = [carve("a", T, S) for _ in range(4)]
        probsT = [carve("a", CK, CHUNKS, T) for _ in range(8)]
        minus_max = carve("a", T, 4)
        oT = carve("b", P, 4, T)
        rden = carve("a", T, H)
        att = carve("b", T, D)
        attT = carve("b", P, DT, T)
        x1 = [carve("b", T, D) for _ in range(2)]
        centred = carve("b", T, D)
        xr_now = carve("b", T, D)
        xrT = carve("b", P, DT, T)
        st1 = carve("b", T, 6)
        mv1 = carve("b", T, 2)
        var1 = carve("b", T, 1)
        rstd = carve("b", T, 1)
        st2 = carve("b", T, 6)
        mv2 = carve("b", T, 2)
        ln2 = carve("b", T, 8)
        zeros = carve("b", P, D)

        w2_sb = arena_a[:, :].rearrange("p (e f d) -> p e f d", e=EXPERTS, f=FT)
        used["b"] = 0
        xs = [carve("b", P, D) for _ in range(2)]
        xsT = carve("b", P, DT, P)
        b1_rep = [carve("b", P, F) for _ in range(2)]
        b2_rep = [carve("b", P, D) for _ in range(2)]
        h_pre = carve("b", P, F)
        h_act = carve("b", P, F)
        hT = carve("b", P, FT, P)
        y_sb = [carve("b", P, D) for _ in range(2)]
        used["b"] = 0
        small = [carve("b", P, B, EXPERTS) for _ in range(9)]
        small_te = carve("b", P, EXPERTS, B)
        small_e = carve("b", P, 12, EXPERTS)
        small_b = carve("b", P, 6, B)
        iota_i = carve("b", P, B * EXPERTS).bitcast(I32)
        upper = carve("b", P, P)
        ones = carve("b", P, P)
        tile_no = carve("b", 1, FFN_TILES, EXPERTS)
        tile_cmp = carve("b", 1, FFN_TILES, EXPERTS)
        tile_sum = carve("b", 1, FFN_TILES)
        used["b"] = 0
        y_got = [carve("b", T, D) for _ in range(8)]
        x1_all = xr_all[:, :, :]

        ps = stack.enter_context(nc.psum_tensor("ps", [P, 8, 512], F32))
        score_bank = [ps[:, 0, :], ps[:, 1, :]]
        probT_bank = [ps[:, 2, :], ps[:, 3, :]]
        out_bank = ps[:, 4, :]
        proj_bank = [ps[:, 5, :], ps[:, 6, :]]
        tail_bank = ps[:, 7, :]

        constants = sem("constants")
        const_dve = sem("const_dve")
        mask_ready = sem("mask_ready")
        weights_loaded = sem("weights_loaded")
        setup_pe = sem("setup_pe")
        setup_copied = sem("setup_copied")
        ctx_loaded = [sem("ctx_loaded0"), sem("ctx_loaded1")]
        x_loaded = [sem("x_loaded0"), sem("x_loaded1")]
        ln1_stats = sem("ln1_stats")
        ln1_mean = sem("ln1_mean")
        ln1_var = sem("ln1_var")
        rstd_ready = sem("rstd_ready")
        xn_ready = sem("xn_ready")
        res_ready = sem("res_ready")
        proj_ready = sem("proj_ready")
        proj_copied = [sem("proj_copied0"), sem("proj_copied1")]
        q1_ready = sem("q1_ready")
        q_masked_ready = sem("q_masked_ready")
        q_parts_ready = sem("q_parts_ready")
        k_high_ready = sem("k_high_ready")
        q_spilled = sem("q_spilled")
        k_spilled = sem("k_spilled")
        q_stacked = [sem("q_stacked0"), sem("q_stacked1")]
        k_stacked = [sem("k_stacked0"), sem("k_stacked1")]
        scores_ready = sem("scores_ready")
        max_ready = sem("max_ready")
        probs_ready = sem("probs_ready")
        probsT_ready = sem("probsT_ready")
        probsT_copied = [sem("probsT_copied_act"), sem("probsT_copied_dve")]
        pv_done = sem("pv_done")
        out_copied = sem("out_copied")
        rden_ready = sem("rden_ready")
        tail_ready = sem("tail_ready")
        tail_copied = sem("tail_copied")
        x1_spilled = [sem("x1_spilled0"), sem("x1_spilled1")]
        ln2_stats = sem("ln2_stats")
        ln2_mean = sem("ln2_mean")
        ln2_chain = sem("ln2_chain")
        centred_ready = sem("centred_ready")
        xr_ready = sem("xr_ready")
        zeroed = sem("zeroed")
        w1_loaded = sem("w1_loaded")
        w2_loaded = sem("w2_loaded")
        route = sem("route")
        route_iota = sem("route_iota")
        route_exp = sem("route_exp")
        ranks_ready = sem("ranks_ready")
        scattered = sem("scattered")
        xs_loaded = [sem("xs_loaded0"), sem("xs_loaded1")]
        b1_loaded = [sem("b1_loaded0"), sem("b1_loaded1")]
        b2_loaded = [sem("b2_loaded0"), sem("b2_loaded1")]
        xsT_ready = sem("xsT_ready")
        xsT_copied = sem("xsT_copied")
        h_ready = sem("h_ready")
        h_biased = sem("h_biased")
        h_activated = sem("h_activated")
        hT_ready = sem("hT_ready")
        hT_copied = [sem("hT_copied_act"), sem("hT_copied_dve")]
        y_ready = sem("y_ready")
        y_biased = sem("y_biased")
        y_stored = [sem("y_stored0"), sem("y_stored1")]
        x1_loaded = sem("x1_loaded")
        gathered = [sem(f"gathered{i}") for i in range(8)]
        combined = sem("combined")
        out_stored = sem("out_stored")

        dve_passed = sem("dve_passed")
        sp_passed = sem("sp_passed")

        block = stack.enter_context(nc.Block())

        N_WEIGHTS = 9 + 2 * PAIRS
        Q_MOVED, K_MOVED = 16 * 2, 16 * len(GROUPS)
        N_CONST_POOL = 3
        N_CONST_DVE = 12

        @block.sync
        def _(sp):
            def load_batch(b, parity):
                sp.dma_start(ctx_in[parity], ctx[bass.ds(b, 1)].rearrange(
                    "o (c k) d -> k (o c) d", c=CHUNKS)).then_inc(ctx_loaded[parity], 16)
                sp.dma_start(x_in[parity], x[bass.ds(b, 1)].rearrange(
                    "o t d -> t (o d)")).then_inc(x_loaded[parity], 16)

            load_batch(0, 0)
            for dst, src in ((wk_in, wk), (wv_sb, wv), (wq_in, wq), (wo_sb, wo)):
                sp.dma_start(dst, src.rearrange("(t p) n -> p t n", p=P)).then_inc(weights_loaded, 16)
            sp.dma_start(bv_cols, bv.rearrange("(t p) -> p t", p=P),
                         allow_slow_non_contiguous=True).then_inc(weights_loaded, 16)
            sp.dma_start(mask_bias, mask.rearrange("a b t s -> (a b t) s")).then_inc(weights_loaded, 16)
            sp.dma_start(bvo, bo.partition_broadcast(T)).then_inc(weights_loaded, 16)
            sp.dma_start(rmsw, rms_w.partition_broadcast(T)).then_inc(weights_loaded, 16)
            sp.dma_start(gw_rows, gate_w).then_inc(weights_loaded, 16)
            load_batch(1, 1)
            sp.wait_ge(constants, N_CONST_POOL)
            sp.dma_start(sorted_rows.rearrange("(n p) d -> p n d", p=P),
                         zeros.unsqueeze(1).to_broadcast([P, FFN_TILES, D])).then_inc(zeroed, 16)
            for e in range(EXPERTS):
                sp.dma_start(w1_sb[:, e], w1[e].rearrange("(t p) f -> p t f", p=P)).then_inc(w1_loaded, 16)

            def step(st):
                if st.exists(0) and st.exists(-2):
                    wait_apart(sp, proj_ready, 8 * st.batch(0) + 2, sp_passed)
                    wait_apart(sp, res_ready, st.batch(0) + 1, sp_passed)
                    load_batch(st.batch(-2), st.parity(-2))
                if st.exists(-1):
                    b, par = st.batch(-1), st.parity(-1)
                    wait_count(sp, scores_ready, H * (b - 1) if st.in_loop or b >= 2 else 0)
                    wait_apart(sp, q_parts_ready, b + 1, sp_passed)
                    sp.dma_start(q_spill[par].rearrange("s p n -> p s n"),
                                 q_parts.rearrange("p s j a t -> p s (j a t)")).then_inc(q_spilled, 16)
                    sp.wait_ge(proj_copied[0], 4 * b + 3)
                    wait_apart(sp, proj_copied[1], 4 * b + 3, sp_passed)
                    sp.dma_start(k_spill[par].rearrange("s p n -> p s n"),
                                 k_parts.rearrange("p s j k -> p s (j k)")).then_inc(k_spilled, 16)
                    sp.wait_ge(q_spilled, 16 * (b + 1))
                    for g in (0, 2):
                        sp.dma_start(q_stack[par][32 * g:32 * g + 64].rearrange("p r j a t -> p (r j a t)"),
                                     q_spill[par].rearrange("s (i r) n -> (s i) (r n)", r=PAIRS)
                                     ).then_inc(q_stacked[par], 16)
                    sp.wait_ge(k_spilled, 16 * (b + 1))
                    for g, (part, _) in enumerate(GROUPS):
                        sp.dma_start(k_stack[par][32 * g:32 * g + 32].rearrange("p r j k -> p (r j k)"),
                                     k_spill[par][part].rearrange("(i r) n -> i (r n)", r=PAIRS)
                                     ).then_inc(k_stacked[par], 16)
                if st.exists(1):
                    sp.wait_ge(tail_copied, 5 * st.batch(1) + 3)
                    sp.dma_start(x1_rows[bass.ds(st.batch(1), 1)].rearrange("o t d -> t (o d)"),
                                 x1[st.parity(1)]).then_inc(x1_spilled[st.parity(1)], 16)

            run_steps(sp, step)

            sp.wait_ge(tail_copied, 5 * B)
            sp.wait_ge(xr_ready, 2 * B)
            sp.wait_ge(x1_spilled[0], 16 * B // 2)
            sp.wait_ge(x1_spilled[1], 16 * B // 2)
            for e in range(EXPERTS):
                sp.dma_start(w2_sb[:, e], w2[e].rearrange("(t p) d -> p t d", p=P)).then_inc(w2_loaded, 16)
            sp.wait_ge(scattered, 16 * B)
            sp.dma_start(x1_all, x1_rows.rearrange("b t d -> t b d")).then_inc(x1_loaded, 16)

            def load_rows(t, parity):
                sp.dma_start(xs[parity], sorted_rows[bass.ds(t * P, P), :]).then_inc(xs_loaded[parity], 16)

            def load_b1(t, parity):
                e = sp.value_load(tile_expert[0:1, bass.ds(t, 1)], min_val=0, max_val=EXPERTS - 1)
                sp.dma_start(b1_rep[parity], b1[bass.ds(e, 1), :].rearrange("o f -> (o f)").partition_broadcast(P)
                             ).then_inc(b1_loaded[parity], 16)

            def load_b2(t, parity):
                e = sp.value_load(tile_expert[0:1, bass.ds(t, 1)], min_val=0, max_val=EXPERTS - 1)
                sp.dma_start(b2_rep[parity], b2[bass.ds(e, 1), :].rearrange("o f -> (o f)").partition_broadcast(P)
                             ).then_inc(b2_loaded[parity], 16)

            def tile_io(t, parity, more):
                if more:
                    sp.wait_ge(xsT_ready, t + 1)
                    load_rows(t + 2, parity)
                    wait_apart(sp, h_biased, t + 1, sp_passed)
                    load_b1(t + 2, parity)
                wait_apart(sp, y_biased, t + 1, sp_passed)
                sp.dma_start(sorted_y[bass.ds(t * P, P), :], y_sb[parity]).then_inc(y_stored[parity], 16)
                if more:
                    load_b2(t + 2, parity)

            for t in range(2):
                load_rows(t, t)
                load_b1(t, t)
                load_b2(t, t)
            with sp.Fori(0, (FFN_TILES - 3) // 2) as i:
                for k in range(2):
                    tile_io(2 * i + k, k, True)
            for t in range(FFN_TILES - 3, FFN_TILES):
                tile_io(t, t % 2, t + 2 < FFN_TILES)
            for b in range(B):
                sp.wait_ge(combined, b + 1)
                sp.dma_start(out[b], x1_all[:, b, :]).then_inc(out_stored, 16)
            sp.wait_ge(out_stored, 16 * B)

        @block.gpsimd
        def _(pool):
            pool.memset(ident[:, :], 0.0).then_inc(constants, 1)
            pool.memset(zeros, 0.0).then_inc(constants, 1)
            pool.wait_ge(constants, 2)
            pool.affine_select(out=ident[:, :], in_=ident[:, :], compare_op=ALU.not_equal, fill=1.0,
                               base=0, pattern=[[-1, P]], channel_multiplier=1).then_inc(constants, 1)
            pool.wait_ge(constants, N_CONST_POOL)
            pool.wait_ge(const_dve, N_CONST_DVE)

            def queries_rstd(b):
                wait_count(pool, xn_ready, b)
                pool.wait_ge(ln1_mean, b + 1)
                pool.tensor_tensor(var1, mv1[:, 1:2], eps_ln, ALU.add).then_inc(ln1_var, 1)
                pool.wait_ge(ln1_var, b + 1)
                pool.tensor_tensor(rstd, var1, minus_half, ALU.pow).then_inc(rstd_ready, 1)

            def step(st):
                if st.exists(2):
                    b = st.batch(2)
                    wait_count(pool, tail_copied, 5 * b)
                    pool.wait_ge(centred_ready, b + 1)
                    pool.tensor_tensor(xr_now, centred, rmsw, ALU.mult).then_inc(xr_ready, 1)
                    pool.tensor_tensor(xr_all[:, bass.ds(b, 1), :].rearrange("p o d -> p (o d)"),
                                       centred, rmsw, ALU.mult).then_inc(xr_ready, 1)
                if st.exists(-1):
                    b, par = st.batch(-1), st.parity(-1)
                    pool.wait_ge(q1_ready, b + 1)
                    pool.wait_ge(proj_copied[1], 4 * b + 2)
                    if st.exists(0):
                        pool.wait_ge(q_spilled, 16 * b)
                    q_both = q1.unsqueeze(2).to_broadcast([P, DT, 2, T])
                    rows = pair_rows.unsqueeze(1).unsqueeze(3).to_broadcast([P, DT, 2, T])
                    pool.tensor_tensor(q_masked, q_both, rows, ALU.mult).then_inc(q_masked_ready, 1)
                    pool.tensor_tensor(q_parts[:, 0], q_both, rows, ALU.mult).then_inc(q_masked_ready, 1)
                    pool.wait_ge(q_masked_ready, 2 * (b + 1))
                    pool.tensor_tensor(q_parts[:, 1], q_masked, q_parts[:, 0], ALU.subtract).then_inc(q_parts_ready, 1)
                if st.exists(-2):
                    queries_rstd(st.batch(-2))
                if st.exists(1):
                    b = st.batch(1)
                    c = 7 * b
                    wait_count(pool, centred_ready, b)
                    pool.wait_ge(ln2_mean, b + 1)
                    for k, a0, a1, op in ((0, mv2[:, 1:2], eps_ln, ALU.add),
                                          (1, ln2[:, 0:1], minus_half, ALU.pow),
                                          (2, mv2[:, 1:2], ln2[:, 1:2], ALU.mult),
                                          (3, ln2[:, 2:3], ln2[:, 1:2], ALU.mult),
                                          (4, ln2[:, 3:4], eps_rms, ALU.add),
                                          (5, ln2[:, 4:5], minus_half, ALU.pow),
                                          (6, ln2[:, 5:6], ln2[:, 1:2], ALU.mult)):
                        pool.tensor_tensor(ln2[:, k:k + 1], a0, a1, op).then_inc(ln2_chain, 1)
                        pool.wait_ge(ln2_chain, c + k + 1)
                if st.exists(-1):
                    b, par = st.batch(-1), st.parity(-1)
                    if st.exists(1):
                        pool.wait_ge(tail_copied, 5 * st.batch(1) + 3)
                    pool.wait_ge(xn_ready, b + 1)
                    pool.tensor_tensor(x_res[par], x_in[par], bvo, ALU.add).then_inc(res_ready, 1)

            pool.wait_ge(setup_copied, 2)
            queries_rstd(0)
            run_steps(pool, step)

            pool.wait_ge(tail_copied, 5 * B)
            pool.wait_ge(xr_ready, 2 * B)
            pool.wait_ge(zeroed, 16)
            pool.iota(iota_i.rearrange("p (b e) -> p b e", b=B), pattern=[[0, B], [-1, EXPERTS]], base=EXPERTS,
                      channel_multiplier=0).then_inc(route_iota, 1)
            pool.wait_ge(route_iota, 1)
            pool.tensor_copy(small[0], iota_i.rearrange("p (b e) -> p b e", b=B)).then_inc(route_iota, 1)
            pool.wait_ge(route_iota, 2)
            pool.iota(iota_i.rearrange("p (e j) -> p e j", e=EXPERTS), pattern=[[0, EXPERTS], [P, B]], base=0,
                      channel_multiplier=0).then_inc(route_iota, 1)
            pool.wait_ge(route_iota, 3)
            pool.tensor_copy(small_te, iota_i.rearrange("p (e j) -> p e j", e=EXPERTS)).then_inc(route_iota, 1)
            pool.memset(upper, 1.0).then_inc(route_iota, 1)
            pool.memset(ones, 1.0).then_inc(route_iota, 1)
            pool.wait_ge(route_iota, 6)
            pool.affine_select(out=upper, in_=upper, compare_op=ALU.is_gt, fill=0.0,
                               base=0, pattern=[[1, P]], channel_multiplier=-1).then_inc(route_iota, 1)
            n = FFN_TILES * EXPERTS
            iota_t = small[8].rearrange("p b e -> p (b e)")
            pool.iota(iota_i[0:1, 0:B * EXPERTS].rearrange("p (t e) -> p t e", e=EXPERTS),
                      pattern=[[1, B], [0, EXPERTS]], base=0, channel_multiplier=0).then_inc(route_iota, 1)
            pool.wait_ge(route_iota, 8)
            pool.tensor_copy(tile_no[:, 0:B, :],
                             iota_i[0:1, 0:B * EXPERTS].rearrange("p (t e) -> p t e", e=EXPERTS)).then_inc(route_iota, 1)
            pool.wait_ge(route_iota, 9)
            left = FFN_TILES - B
            pool.iota(iota_i[0:1, 0:left * EXPERTS].rearrange("p (t e) -> p t e", e=EXPERTS),
                      pattern=[[1, left], [0, EXPERTS]], base=B, channel_multiplier=0).then_inc(route_iota, 1)
            pool.wait_ge(route_iota, 10)
            pool.tensor_copy(tile_no[:, B:FFN_TILES, :],
                             iota_i[0:1, 0:left * EXPERTS].rearrange("p (t e) -> p t e", e=EXPERTS)
                             ).then_inc(route_iota, 1)
            pool.wait_ge(route, N_ROUTE)
            for b in range(B):
                pool.indirect_dma_start(out=sorted_rows, out_offset=bass.IndirectOffsetOnAxis(ap=slot_of[:, b:b + 1], axis=0),
                                        in_=xr_all[:, b, :], in_offset=None).then_inc(scattered, 16)
            pool.wait_ge(y_stored[0], 16 * ((FFN_TILES + 1) // 2))
            pool.wait_ge(y_stored[1], 16 * (FFN_TILES // 2))
            for b in range(B):
                if b >= 8:
                    pool.wait_ge(combined, b - 7)
                pool.indirect_dma_start(out=y_got[b % 8], out_offset=None, in_=sorted_y,
                                        in_offset=bass.IndirectOffsetOnAxis(ap=slot_of[:, b:b + 1], axis=0)
                                        ).then_inc(gathered[b % 8], 16)

        @block.scalar
        def _(act):
            for dst, src in ((bk_sb, bk), (bq_sb, bq)):
                for r in range(PAIRS):
                    act.dma_start(dst[r:P:PAIRS], src.rearrange("(j r i) -> r i j", r=PAIRS, i=32)[r],
                                  allow_slow_non_contiguous=True).then_inc(weights_loaded, 16)
            act.wait_ge(setup_pe, 1)
            nc.scalar.activation(gw_sb, tail_bank[:, 0:DT * EXPERTS].rearrange("p (t e) -> p t e", t=DT),
                                 ACT.Copy).then_inc(setup_copied, 1)

            def copy_probsT(lag, head):
                act.wait_ge(probsT_ready, H * st_.batch(lag) + head + 1)
                slot_free(act, lag, head)
                nc.scalar.activation(probsT[head % 8], probT_bank[head % 2][0:CK, 0:CHUNKS * T].rearrange(
                    "p (c t) -> p c t", c=CHUNKS), ACT.Copy).then_inc(probsT_copied[0], 1)

            def slot_free(eng, lag, head):
                quads = 4 * st_.batch(lag) + head // 4 - 1
                wait_count(eng, pv_done, quads)

            def step(st):
                nonlocal st_
                st_ = st
                for slot in range(H):
                    lag, head = (0, slot - HEAD_LAG_COPY) if slot >= HEAD_LAG_COPY else (1, H + slot - HEAD_LAG_COPY)
                    if head % 2 == 0 and st.exists(lag):
                        copy_probsT(lag, head)
                    if st.exists(-1):
                        b, par = st.batch(-1), st.parity(-1)
                        if slot in (1, 2):
                            j = slot - 1
                            act.wait_ge(proj_ready, 8 * b + 1 + j)
                            nc.scalar.activation(ctxT[:, j, :], proj_bank[j][:, 0:S], ACT.Copy
                                                 ).then_inc(proj_copied[j], 1)
                        if slot in (7, 8):
                            j = slot - 7
                            act.wait_ge(proj_ready, 8 * b + 5 + j)
                            if st.exists(0):
                                act.wait_ge(k_spilled, 16 * b)
                            nc.scalar.activation(k_parts[:, 0, j, :], proj_bank[j][:, 0:S], ACT.Identity,
                                                 bias=bk_sb[:, j:j + 1]).then_inc(k_high_ready, 1)
                        if slot in (12, 13):
                            j = slot - 12
                            act.wait_ge(proj_ready, 8 * b + 7 + j)
                            wait_count(act, pv_done, 4 * (b - 1) if st.in_loop or b >= 1 else 0)
                            n = 2 - j
                            nc.scalar.activation(
                                v_aug[par][:, 2 * j:2 * j + n, :, 0:DH],
                                proj_bank[j][0:CK, 0:n * D].rearrange("p (c h d) -> p c h d", c=n, h=H),
                                ACT.Copy).then_inc(proj_copied[j], 1)
                        if slot == 3:
                            act.wait_ge(proj_ready, 8 * b + 3)
                            nc.scalar.activation(xnT, proj_bank[0][:, 0:DT * T].rearrange("p (j t) -> p j t", j=DT),
                                                 ACT.Copy).then_inc(proj_copied[0], 1)
                    if st.exists(1):
                        b = st.batch(1)
                        if slot == 6:
                            act.wait_ge(pv_done, 4 * b + 4)
                            wait_count(act, tail_ready, 5 * b - 4 if st.in_loop or b >= 1 else 0)
                            nc.scalar.activation(oT, out_bank[:, 0:4 * T].rearrange("p (g t) -> p g t", g=4),
                                                 ACT.Copy).then_inc(out_copied, 1)
                        if slot == 13:
                            act.wait_ge(tail_ready, 5 * b + 2)
                            nc.scalar.activation(attT, tail_bank[:, 0:DT * T].rearrange("p (j t) -> p j t", j=DT),
                                                 ACT.Copy).then_inc(tail_copied, 1)
                    if st.exists(2) and slot == 6:
                        act.wait_ge(tail_ready, 5 * st.batch(2) + 4)
                        nc.scalar.activation(xrT, tail_bank[:, 0:DT * T].rearrange("p (j t) -> p j t", j=DT),
                                             ACT.Copy).then_inc(tail_copied, 1)
                    if st.exists(0):
                        act.wait_ge(max_ready, H * st.batch(0) + slot + 1)
                        nc.scalar.activation(probs[slot % 4], probs[slot % 4], ACT.Exp,
                                             bias=minus_max[:, slot % 4:slot % 4 + 1], scale=-1.0
                                             ).then_inc(probs_ready, 1)

            st_ = None
            run_steps(act, step)
            act.wait_ge(route, R_DIFF)
            nc.scalar.activation(small[2][0:T], small[1][0:T], ACT.Exp).then_inc(route_exp, 1)

            def copy_xsT(t):
                act.wait_ge(xsT_ready, t + 1)
                nc.scalar.activation(xsT, ps[:, 0, 0:DT * P].rearrange("p (j t) -> p j t", j=DT),
                                     ACT.Copy).then_inc(xsT_copied, 1)

            def tile_steps(t, first, last):
                act.wait_ge(h_biased, t + 1)
                if not first:
                    act.wait_ge(hT_ready, 2 * t)
                nc.scalar.activation(h_act, h_pre, ACT.Silu).then_inc(h_activated, 1)
                if not last:
                    copy_xsT(t + 1)
                act.wait_ge(hT_ready, 2 * t + 1)
                if not first:
                    act.wait_ge(y_ready, t)
                nc.scalar.activation(hT[:, 0:FT // 2, :], ps[:, 3, :].rearrange("p (f t) -> p f t", t=P),
                                     ACT.Copy).then_inc(hT_copied[0], 1)

            act.wait_ge(scattered, 16 * B)
            copy_xsT(0)
            tile_steps(0, True, False)
            with act.Fori(1, FFN_TILES - 1) as t:
                tile_steps(t, False, False)
            tile_steps(FFN_TILES - 1, False, True)

        @block.tensor
        def _(pe):
            pe.wait_ge(constants, N_CONST_POOL)
            pe.wait_ge(weights_loaded, 16 * N_WEIGHTS)
            for j in range(DT):
                mm = pe.transpose(tail_bank[:, j * EXPERTS:(j + 1) * EXPERTS], gw_rows[:, j * P:(j + 1) * P],
                                  ident[0:EXPERTS, 0:EXPERTS])
            mm.then_inc(setup_pe, 1)
            pe.wait_ge(const_dve, N_CONST_DVE)
            for j in range(DT):
                mm = pe.matmul(proj_bank[0][0:T, 0:D], bv_rep[:, j, :], wo_sb[:, j, :], start=j == 0, stop=j == DT - 1)
            mm.then_inc(setup_pe, 1)
            pe.wait_ge(setup_copied, 2)

            def scores(st, head):
                b = st.batch(0)
                if head == 0:
                    pe.wait_ge(q_stacked[st.parity(0)], Q_MOVED * (st.half(0) + 1))
                    pe.wait_ge(k_stacked[st.parity(0)], K_MOVED * (st.half(0) + 1))
                wait_count(pe, max_ready, H * b + head - 1)
                j, r, a = head // HPT, head % HPT // 2, head % 2
                pe.matmul(score_bank[head % 2][0:T, 0:S], q_stack[st.parity(0)][:, r, j, a, :],
                          k_stack[st.parity(0)][:, r, j, :], start=True, stop=True).then_inc(scores_ready, 1)

            def transpose_probs(st, lag, head):
                b = st.batch(lag)
                wait_count(pe, probsT_copied[head % 2], 8 * b + head // 2)
                pe.wait_ge(probs_ready, H * b + head + 1)
                for c in range(CHUNKS):
                    mm = pe.transpose(probT_bank[head % 2][0:CK, c * T:(c + 1) * T],
                                      probs[head % 4][:, c * CK:(c + 1) * CK], ident[0:T, 0:T])
                mm.then_inc(probsT_ready, 1)

            def values(st, lag, quad):
                b, par = st.batch(lag), st.parity(lag)
                if quad == 0:
                    pe.wait_ge(proj_copied[0], 4 * b + 4)
                    pe.wait_ge(proj_copied[1], 4 * b + 4)
                    wait_count(pe, out_copied, b)
                pe.wait_ge(probsT_copied[0], 8 * b + 2 * quad + 2)
                pe.wait_ge(probsT_copied[1], 8 * b + 2 * quad + 2)
                for c in range(CHUNKS):
                    for r in range(4):
                        head = 4 * quad + r
                        mm = pe.matmul(out_bank[32 * r:32 * r + VW, quad * T:(quad + 1) * T],
                                       v_aug[par][:, c, head, :], probsT[head % 8][:, c, :],
                                       start=c == 0, stop=c == CHUNKS - 1)
                mm.then_inc(pv_done, 1)

            def projections(st, slot):
                b, par = st.batch(-1), st.parity(-1)
                if slot in (0, 1):
                    if slot == 0:
                        pe.wait_ge(ctx_loaded[par], 16 * (st.half(-1) + 1))
                    wait_count(pe, proj_copied[slot], 4 * b)
                    for c in range(CHUNKS):
                        mm = pe.transpose(proj_bank[slot][:, c * CK:(c + 1) * CK],
                                          ctx_in[par][:, c, slot * P:(slot + 1) * P], ident[0:CK, 0:CK])
                    mm.then_inc(proj_ready, 1)
                if slot in (6, 7):
                    j = slot - 6
                    pe.wait_ge(proj_copied[0], 4 * b + 2)
                    pe.wait_ge(proj_copied[1], 4 * b + 1 + j)
                    for k in range(DT):
                        mm = pe.matmul(proj_bank[j][:, 0:S], wk_sb[:, k, j * P:(j + 1) * P], ctxT[:, k, :],
                                       start=k == 0, stop=k == DT - 1)
                    mm.then_inc(proj_ready, 1)
                if slot in (10, 11, 12):
                    c = slot - 10
                    if c % 2 == 0:
                        pe.wait_ge(proj_copied[c // 2], 4 * b + 3)
                    for k in range(DT):
                        mm = pe.matmul(proj_bank[c // 2][0:CK, (c % 2) * D:(c % 2 + 1) * D],
                                       ctxT[:, k, c * CK:(c + 1) * CK], wv_sb[:, k, :],
                                       start=k == 0, stop=k == DT - 1)
                    if c > 0:
                        mm.then_inc(proj_ready, 1)
                if slot == 2:
                    pe.wait_ge(proj_copied[0], 4 * b + 1)
                    pe.wait_ge(xn_ready, b + 1)
                    for j in range(DT):
                        mm = pe.transpose(proj_bank[0][:, j * T:(j + 1) * T], xn[:, j * P:(j + 1) * P], ident[0:T, 0:T])
                    mm.then_inc(proj_ready, 1)
                if slot == 4:
                    pe.wait_ge(proj_copied[1], 4 * b + 1)
                    pe.wait_ge(proj_copied[0], 4 * b + 2)
                    for j in range(DT):
                        for k in range(DT):
                            mm = pe.matmul(proj_bank[1][:, j * T:(j + 1) * T], wq_sb[:, k, j * P:(j + 1) * P],
                                           xnT[:, k, :], start=k == 0, stop=k == DT - 1)
                    mm.then_inc(proj_ready, 1)

            def tail(st, slot):
                if st.exists(2) and slot in (5, 8):
                    b = st.batch(2)
                    if slot == 5:
                        pe.wait_ge(tail_copied, 5 * b + 3)
                        pe.wait_ge(xr_ready, 2 * b + 1)
                        for j in range(DT):
                            mm = pe.transpose(tail_bank[:, j * T:(j + 1) * T], xr_now[:, j * P:(j + 1) * P],
                                              ident[0:T, 0:T])
                        mm.then_inc(tail_ready, 1)
                    else:
                        pe.wait_ge(tail_copied, 5 * b + 4)
                        for j in range(DT):
                            mm = pe.matmul(tail_bank[0:T, 0:EXPERTS], xrT[:, j, :], gw_sb[:, j, :],
                                           start=j == 0, stop=j == DT - 1)
                        mm.then_inc(tail_ready, 1)
                if st.exists(1) and slot in (10, 12, 14):
                    b = st.batch(1)
                    if slot == 10:
                        wait_count(pe, tail_copied, 5 * b)
                        pe.wait_ge(out_copied, b + 1)
                        for g in range(4):
                            mm = pe.transpose(tail_bank[0:T, g * P:(g + 1) * P], oT[:, g, :], ident[:, :])
                        mm.then_inc(tail_ready, 1)
                    elif slot == 12:
                        pe.wait_ge(tail_copied, 5 * b + 1)
                        for j in range(DT):
                            mm = pe.transpose(tail_bank[:, j * T:(j + 1) * T], att[:, j * P:(j + 1) * P], ident[0:T, 0:T])
                        mm.then_inc(tail_ready, 1)
                    else:
                        pe.wait_ge(tail_copied, 5 * b + 2)
                        for j in range(DT):
                            mm = pe.matmul(tail_bank[0:T, 0:D], attT[:, j, :], wo_sb[:, j, :],
                                           start=j == 0, stop=j == DT - 1)
                        mm.then_inc(tail_ready, 1)

            def step(st):
                for slot in range(H):
                    if st.exists(0):
                        scores(st, slot)
                    lag, head = (0, slot - HEAD_LAG_T) if slot >= HEAD_LAG_T else (1, H + slot - HEAD_LAG_T)
                    if st.exists(lag):
                        transpose_probs(st, lag, head)
                    if slot % 4 == 1:
                        lag, quad = (0, (slot - 9) // 4) if slot >= 9 else (1, 2 + slot // 4)
                        if st.exists(lag):
                            values(st, lag, quad)
                    if st.exists(-1):
                        projections(st, slot)
                    tail(st, slot)

            run_steps(pe, step)

            pe.wait_ge(route_iota, 7)
            pe.wait_ge(route, R_ONEHOT)
            pe.matmul(ps[0:T, 0, 0:B * EXPERTS], upper[0:T, 0:T], small[3][0:T].rearrange("p b e -> p (b e)"),
                      start=True, stop=True).then_inc(ranks_ready, 1)
            pe.matmul(ps[:, 1, 0:B * EXPERTS], ones[0:T, :], small[3][0:T].rearrange("p b e -> p (b e)"),
                      start=True, stop=True).then_inc(ranks_ready, 1)

            def transpose_rows(t, parity, half):
                pe.wait_ge(xs_loaded[parity], 16 * (half + 1))
                for j in range(DT):
                    mm = pe.transpose(ps[:, 0, j * P:(j + 1) * P], xs[parity][:, j * P:(j + 1) * P], ident[:, :])
                mm.then_inc(xsT_ready, 1)

            def hidden(t, first):
                e = pe.value_load(tile_expert[0:1, bass.ds(t, 1)], min_val=0, max_val=EXPERTS - 1)
                if not first:
                    pe.wait_ge(h_biased, t)
                pe.wait_ge(xsT_copied, t + 1)
                for n in range(2):
                    for k in range(DT):
                        mm = pe.matmul(ps[:, 1 + n, :], xsT[:, k, :],
                                       w1_sb[:, bass.ds(e, 1), k, n * 512:(n + 1) * 512].rearrange("p o f -> p (o f)"),
                                       start=k == 0, stop=k == DT - 1)
                mm.then_inc(h_ready, 1)

            def transpose_hidden(t, first):
                pe.wait_ge(h_activated, t + 1)
                if not first:
                    pe.wait_ge(hT_copied[0], t)
                    pe.wait_ge(hT_copied[1], t)
                for f in range(FT):
                    mm = pe.transpose(ps[:, 3 + f // 4, (f % 4) * P:(f % 4 + 1) * P], h_act[:, f * P:(f + 1) * P],
                                      ident[:, :])
                    if f % 4 == 3:
                        mm.then_inc(hT_ready, 1)

            def outputs(t, first):
                e = pe.value_load(tile_expert[0:1, bass.ds(t, 1)], min_val=0, max_val=EXPERTS - 1)
                if not first:
                    pe.wait_ge(y_biased, t)
                pe.wait_ge(hT_copied[0], t + 1)
                pe.wait_ge(hT_copied[1], t + 1)
                for f in range(FT):
                    mm = pe.matmul(ps[:, 5, 0:D], hT[:, f, :],
                                   w2_sb[:, bass.ds(e, 1), f, :].rearrange("p o d -> p (o d)"),
                                   start=f == 0, stop=f == FT - 1)
                mm.then_inc(y_ready, 1)

            pe.wait_ge(route, N_ROUTE)
            pe.wait_ge(w1_loaded, 16 * EXPERTS)
            transpose_rows(0, 0, 0)
            hidden(0, True)
            transpose_rows(1, 1, 0)
            pe.wait_ge(w2_loaded, 16 * EXPERTS)
            transpose_hidden(0, True)
            hidden(1, False)
            outputs(0, True)
            transpose_rows(2, 0, 1)
            with pe.Fori(0, (FFN_TILES - 3) // 2) as i:
                for k in range(2):
                    t = 2 * i + 2 + k
                    transpose_hidden(t - 1, False)
                    hidden(t, False)
                    outputs(t - 1, False)
                    transpose_rows(t + 1, (k + 1) % 2, i + 1 + (k + 1) // 2)
            t = FFN_TILES - 1
            transpose_hidden(t - 1, False)
            hidden(t, False)
            outputs(t - 1, False)
            transpose_hidden(t, False)
            outputs(t, False)

        @block.vector
        def _(dve):
            dve.memset(v_aug[0], 1.0).then_inc(const_dve, 1)
            dve.memset(v_aug[1], 1.0).then_inc(const_dve, 1)
            dve.memset(out_bank, 0.0).then_inc(const_dve, 1)
            dve.memset(eps_ln, LN_EPS).then_inc(const_dve, 1)
            dve.memset(eps_rms, RMS_EPS).then_inc(const_dve, 1)
            dve.memset(minus_half, -0.5).then_inc(const_dve, 1)
            dve.wait_ge(weights_loaded, 16 * N_WEIGHTS)
            nc.vector.tensor_copy(bv_rep, bv_cols.unsqueeze(2).to_broadcast([P, DT, T])).then_inc(const_dve, 1)
            for weights, loaded, scale in ((wk_sb, wk_in, SCALE_K), (wq_sb, wq_in, SCALE_Q * DH ** -0.5)):
                nc.vector.tensor_scalar(weights.rearrange("p t (j i r) -> p (t j) i r", i=32, r=PAIRS),
                                        loaded.rearrange("p t (j r i) -> p (t j) i r", i=32, r=PAIRS),
                                        scale, None, ALU.mult).then_inc(const_dve, 1)
            for bias, scale in ((bk_sb, SCALE_K), (bq_sb, SCALE_Q * DH ** -0.5)):
                nc.vector.tensor_scalar(bias, bias, scale, None, ALU.mult).then_inc(const_dve, 1)
            dve.wait_ge(constants, N_CONST_POOL)
            nc.vector.tensor_reduce(pair_rows, ident[:, :].rearrange("p (a i) -> p a i", a=2),
                                    AX_X, ALU.add).then_inc(const_dve, 1)
            nc.vector.tensor_scalar(mask_bias, mask_bias, NEG_BIG, SCALE_SCORES, ALU.mult, ALU.mult
                                    ).then_inc(mask_ready, 1)
            dve.wait_ge(setup_pe, 2)
            nc.vector.tensor_tensor(bvo, proj_bank[0][0:T, 0:D], bvo, ALU.add).then_inc(setup_copied, 1)
            dve.wait_ge(mask_ready, 1)

            def queries_stats(b, parity, half):
                dve.wait_ge(x_loaded[parity], 16 * (half + 1))
                nc.vector.bn_stats(st1, x_in[parity]).then_inc(ln1_stats, 1)
                wait_apart(dve, ln1_stats, b + 1, dve_passed)
                nc.vector.bn_aggr(mv1, st1).then_inc(ln1_mean, 1)

            def step(st):
                for slot in range(H):
                    lag, head = (0, slot - HEAD_LAG_COPY) if slot >= HEAD_LAG_COPY else (1, H + slot - HEAD_LAG_COPY)
                    if head % 2 == 1 and st.exists(lag):
                        dve.wait_ge(probsT_ready, H * st.batch(lag) + head + 1)
                        wait_count(dve, pv_done, 4 * st.batch(lag) + head // 4 - 1)
                        nc.vector.tensor_copy(probsT[head % 8], probT_bank[head % 2][0:CK, 0:CHUNKS * T].rearrange(
                            "p (c t) -> p c t", c=CHUNKS)).then_inc(probsT_copied[1], 1)
                    if st.exists(-1):
                        b, par = st.batch(-1), st.parity(-1)
                        if slot in (8, 9):
                            j = slot - 8
                            dve.wait_ge(k_high_ready, DT * b + j + 1)
                            nc.vector.scalar_tensor_tensor(
                                out=k_parts[:, 1, j, :], in0=proj_bank[j][:, 0:S], scalar=bk_sb[:, j:j + 1],
                                in1=k_parts[:, 0, j, :], op0=ALU.add, op1=ALU.subtract).then_inc(proj_copied[j], 1)
                        if slot == 5:
                            dve.wait_ge(proj_ready, 8 * b + 4)
                            wait_count(dve, q_parts_ready, b)
                            for j, done in ((0, q1_ready), (1, proj_copied[1])):
                                nc.vector.tensor_scalar(q1[:, j, :], proj_bank[1][:, j * T:(j + 1) * T],
                                                        bq_sb[:, j:j + 1], None, ALU.add
                                                        ).then_inc(done, 1)
                    if st.exists(-2) and slot == 12:
                        queries_stats(st.batch(-2), st.parity(-2), st.half(-2))
                    if st.exists(2) and slot == 9:
                        b = st.batch(2)
                        dve.wait_ge(tail_ready, 5 * b + 5)
                        nc.vector.tensor_copy(gate_logits[:, bass.ds(b, 1), :].rearrange("p o e -> p (o e)"),
                                              tail_bank[0:T, 0:EXPERTS]).then_inc(tail_copied, 1)
                    if st.exists(1):
                        b, par = st.batch(1), st.parity(1)
                        if slot == 11:
                            heads = tail_bank[0:T, :].rearrange("p (h w) -> p h w", w=32)
                            dve.wait_ge(tail_ready, 5 * b + 1)
                            nc.vector.reciprocal(rden, heads[:, :, DH]).then_inc(rden_ready, 1)
                            dve.wait_ge(rden_ready, b + 1)
                            nc.vector.tensor_tensor(att.rearrange("p (h d) -> p h d", h=H), heads[:, :, 0:DH],
                                                    rden.unsqueeze(2).to_broadcast([T, H, DH]), ALU.mult
                                                    ).then_inc(tail_copied, 1)
                    if st.exists(2) and slot == 3:
                            b, par = st.batch(2), st.parity(2)
                            wait_count(dve, xr_ready, 2 * b)
                            dve.wait_ge(ln2_chain, 7 * b + 7)
                            nc.vector.tensor_scalar(centred, x1[par], mv2[:, 0:1], ln2[:, 6:7], ALU.subtract,
                                                    ALU.mult).then_inc(centred_ready, 1)
                    if st.exists(0):
                        b = st.batch(0)
                        wait_count(dve, probsT_ready, H * b + slot - 3)
                        wait_apart(dve, scores_ready, H * b + slot + 1, dve_passed)
                        nc.vector.tensor_tensor_reduce(
                            out=probs[slot % 4], in0=score_bank[slot % 2][0:T, 0:S], in1=mask_bias, scale=-1.0 / SCALE_SCORES,
                            scalar=3.4e38, op0=ALU.add, op1=ALU.min,
                            accum_out=minus_max[:, slot % 4:slot % 4 + 1]).then_inc(max_ready, 1)
                    if st.exists(-1):
                        b, par = st.batch(-1), st.parity(-1)
                        if slot == 0:
                            dve.wait_ge(rstd_ready, b + 1)
                            nc.vector.tensor_scalar(xn, x_in[par], mv1[:, 0:1], rstd[:, 0:1], ALU.subtract,
                                                    ALU.mult).then_inc(xn_ready, 1)
                    if st.exists(1):
                        b, par = st.batch(1), st.parity(1)
                        if slot == 15:
                            dve.wait_ge(tail_ready, 5 * b + 3)
                            dve.wait_ge(res_ready, b + 1)
                            wait_count(dve, x1_spilled[par], 16 * st.half(1))
                            nc.vector.tensor_tensor(x1[par], tail_bank[0:T, 0:D], x_res[par], ALU.add
                                                    ).then_inc(tail_copied, 1)
                            dve.wait_ge(tail_copied, 5 * b + 3)
                            nc.vector.bn_stats(st2, x1[par]).then_inc(ln2_stats, 1)
                            wait_apart(dve, ln2_stats, b + 1, dve_passed)
                            nc.vector.bn_aggr(mv2, st2).then_inc(ln2_mean, 1)

            queries_stats(0, 0, 0)
            run_steps(dve, step)

            done = [0]

            def link(instruction):
                done[0] += 1
                instruction.then_inc(route, 1)
                dve.wait_ge(route, done[0])

            def over_experts(ap):
                return ap.unsqueeze(2).to_broadcast([T, B, EXPERTS])

            order, diff, exps, onehot, weighted, rank, counts, scan_a, scan_b = [s for s in small]
            gmax, gsum, emax, wmax, slot_f = [small_b[0:T, i, :] for i in range(5)]
            dve.wait_ge(tail_copied, 5 * B)
            link(nc.vector.tensor_reduce(gmax, gate_logits[:, :, :], AX_X, ALU.max))
            link(nc.vector.tensor_tensor(diff[0:T], gate_logits[:, :, :], over_experts(gmax), ALU.subtract))
            assert done[0] == R_DIFF
            dve.wait_ge(route_exp, 1)
            link(nc.vector.tensor_reduce(gsum, exps[0:T], AX_X, ALU.add))
            link(nc.vector.tensor_reduce(emax, exps[0:T], AX_X, ALU.max))
            link(nc.vector.reciprocal(wmax, gsum))
            link(nc.vector.tensor_tensor(score[:, :], emax, wmax, ALU.mult))
            link(nc.vector.tensor_tensor(weighted[0:T], exps[0:T], over_experts(emax), ALU.is_equal))
            dve.wait_ge(route_iota, 2)
            link(nc.vector.tensor_tensor(weighted[0:T], weighted[0:T], order[0:T], ALU.mult))
            link(nc.vector.tensor_reduce(wmax, weighted[0:T], AX_X, ALU.max))
            link(nc.vector.tensor_tensor(onehot[0:T], weighted[0:T], over_experts(wmax), ALU.is_equal))
            assert done[0] == R_ONEHOT
            dve.wait_ge(ranks_ready, 2)
            link(nc.vector.tensor_copy(rank[0:T], ps[0:T, 0, 0:B * EXPERTS].rearrange("p (b e) -> p b e", b=B)))
            link(nc.vector.tensor_copy(counts, ps[:, 1, 0:B * EXPERTS].rearrange("p (b e) -> p b e", b=B)))
            link(nc.vector.tensor_copy(scan_a, counts))
            a, c = scan_a, scan_b
            for k in (1, 2, 4, 8, 16):
                nc.vector.tensor_copy(c[:, 0:k, :], a[:, 0:k, :])
                link(nc.vector.tensor_tensor(c[:, k:B, :], a[:, k:B, :], a[:, 0:B - k, :], ALU.add))
                a, c = c, a
            total = a[:, B - 1, :]
            dve.wait_ge(route_iota, 11)
            tiles_e, cum0, cum1, start = [small_e[:, i, :] for i in range(4)]
            link(nc.vector.tensor_tensor(small_te, small_te, total.unsqueeze(2).to_broadcast([P, EXPERTS, B]),
                                         ALU.is_lt))
            link(nc.vector.tensor_reduce(tiles_e, small_te, AX_X, ALU.add))
            link(nc.vector.tensor_copy(cum0, tiles_e))
            u, v = cum0, cum1
            for k in (1, 2, 4):
                nc.vector.tensor_copy(v[:, 0:k], u[:, 0:k])
                link(nc.vector.tensor_tensor(v[:, k:EXPERTS], u[:, k:EXPERTS], u[:, 0:EXPERTS - k], ALU.add))
                u, v = v, u
            link(nc.vector.tensor_tensor(start, u, tiles_e, ALU.subtract))
            link(nc.vector.tensor_scalar(start, start, float(P), None, ALU.mult))
            link(nc.vector.tensor_tensor(rank[0:T], rank[0:T], a[0:T], ALU.add))
            link(nc.vector.tensor_tensor(rank[0:T], rank[0:T], counts[0:T], ALU.subtract))
            link(nc.vector.tensor_tensor(rank[0:T], rank[0:T],
                                         start[0:T].unsqueeze(1).to_broadcast([T, B, EXPERTS]), ALU.add))
            link(nc.vector.tensor_tensor(rank[0:T], rank[0:T], onehot[0:T], ALU.mult))
            link(nc.vector.tensor_reduce(slot_f, rank[0:T], AX_X, ALU.add))
            link(nc.vector.tensor_copy(slot_of[:, :], slot_f))
            link(nc.vector.tensor_tensor(tile_cmp, tile_no, u[0:1].unsqueeze(1).to_broadcast([1, FFN_TILES, EXPERTS]),
                                         ALU.is_ge))
            link(nc.vector.tensor_reduce(tile_sum, tile_cmp, AX_X, ALU.add))
            link(nc.vector.tensor_scalar(tile_expert[:, 0:FFN_TILES], tile_sum, float(EXPERTS - 1), None, ALU.min))
            assert done[0] == N_ROUTE, done

            def tile_steps(t, parity, half, first, last_y):
                dve.wait_ge(b1_loaded[parity], 16 * (half + 1))
                if not first:
                    dve.wait_ge(h_activated, t)
                dve.wait_ge(h_ready, t + 1)
                nc.vector.tensor_tensor(h_pre, ps[:, 1:3, :].rearrange("p a b -> p (a b)"), b1_rep[parity],
                                        ALU.add).then_inc(h_biased, 1)

            def add_y(t, parity, half, first2):
                dve.wait_ge(b2_loaded[parity], 16 * (half + 1))
                dve.wait_ge(y_ready, t + 1)
                if not first2:
                    dve.wait_ge(y_stored[parity], 16 * half)
                nc.vector.tensor_tensor(y_sb[parity], ps[:, 5, 0:D], b2_rep[parity], ALU.add).then_inc(y_biased, 1)

            def copy_hT(t, first):
                dve.wait_ge(hT_ready, 2 * t + 2)
                if not first:
                    dve.wait_ge(y_ready, t)
                nc.vector.tensor_copy(hT[:, FT // 2:FT, :], ps[:, 4, :].rearrange("p (f t) -> p f t", t=P)
                                      ).then_inc(hT_copied[1], 1)

            dve.wait_ge(scattered, 16 * B)
            tile_steps(0, 0, 0, True, None)
            copy_hT(0, True)
            tile_steps(1, 1, 0, False, None)
            add_y(0, 0, 0, True)
            copy_hT(1, False)
            tile_steps(2, 0, 1, False, None)
            add_y(1, 1, 0, True)
            with dve.Fori(0, (FFN_TILES - 3) // 2) as i:
                for k in range(2):
                    t = 2 * i + 3 + k
                    copy_hT(t - 1, False)
                    tile_steps(t, (k + 1) % 2, i + 1 + (k + 1) // 2, False, None)
                    add_y(t - 1, k % 2, i + 1 + k // 2, False)
            t = FFN_TILES - 1
            copy_hT(t, False)
            add_y(t, t % 2, t // 2, False)

            dve.wait_ge(x1_loaded, 16)
            for b in range(B):
                dve.wait_ge(gathered[b % 8], 16 * (b // 8 + 1))
                nc.vector.scalar_tensor_tensor(out=x1_all[:, b, :], in0=y_got[b % 8], scalar=score[:, b:b + 1],
                                               in1=x1_all[:, b, :], op0=ALU.mult, op1=ALU.add
                                               ).then_inc(combined, 1)


R_DIFF, R_ONEHOT, N_ROUTE = 2, 10, 35

_INS = ["x", "ctx_1024", "mask_1x1xSxS2_fk1", "L0_xattn_wq_w", "L0_xattn_wq_b", "L0_xattn_wk_w", "L0_xattn_wk_b",
        "L0_xattn_wv_w", "L0_xattn_wv_b", "L0_xattn_wo_w", "L0_xattn_wo_b", "L0_ffn_rms_w", "L0_ffn_gate_w",
        "L0_ffn_W1", "L0_ffn_b1", "L0_ffn_W2", "L0_ffn_b2"]


def kernel(**inputs):
    import numpy as np
    import concourse.bacc as bacc
    from concourse.bass_utils import run_bass_kernel_spmd

    nc = bacc.Bacc("TRN2", target_bir_lowering=False, num_devices=1)
    arrays, args = {}, []
    for name in _INS:
        a = np.ascontiguousarray(inputs[name])
        arrays[f"in_{name}"] = a
        args.append(nc.dram_tensor(f"in_{name}", a.shape, mybir.dt.from_np(a.dtype), kind="ExternalInput").ap())
    out = nc.dram_tensor("out", (B, T, D), F32, kind="ExternalOutput").ap()
    build(nc, *args, out)
    r = run_bass_kernel_spmd(nc, [arrays], core_ids=[0])
    return r.results[0]["out"]
```

```python
from contextlib import ExitStack

import concourse.bass as bass
from concourse import mybir

ALU = mybir.AluOpType
ACT = mybir.ActivationFunctionType
F32 = mybir.dt.float32
F16 = mybir.dt.float16
I32 = mybir.dt.int32
U32 = mybir.dt.uint32
AX_X = mybir.AxisListType.X

P = 128
B, T, D = 32, 112, 256
S, CHUNKS = 375, 3
CK = S // CHUNKS
H = 16
DH = D // H
DT = D // P
HPT = H // DT
VW = DH + 1
NEG_BIG = -1e9
EXPERTS, F = 8, 1024
FT = F // P
FFN_TILES = (B * T + EXPERTS * (P - 1)) // P
GROUPS = ((0, 0), (0, 1), (1, 0), (1, 1))
PAIRS = P // (2 * DH)
SCALE_K, SCALE_Q, SCALE_V = 64.0, 64.0, 64.0
SCALE_SCORES = SCALE_K * SCALE_Q
SCALE_W, SCALE_X = 256.0, 64.0
PASSES = ((0, 0), (0, 1), (1, 0))
ROW, NO_TOKEN = D + 2, 8192
FFN_UNROLL = 4
FFN_PEELED = 3
FFN_LOOPS = (FFN_TILES - FFN_PEELED - 1) // FFN_UNROLL
W_CHUNK = EXPERTS * DT * F // B
LN_EPS, RMS_EPS = 1e-5, 1e-6
HEAD_LAG_T, HEAD_LAG_COPY = 3, 4
VALUES_SLOTS = (7, 8, 10)
CONTEXT_SLOTS = (11, 12)
PEELED_FIRST, UNROLL = 4, 2


class Step:

    def __init__(self, base, i=0, in_loop=False):
        self.base, self.i, self.in_loop = base, i, in_loop

    def batch(self, lag):
        return self.i * UNROLL + (self.base - lag) if self.in_loop else self.base - lag

    def exists(self, lag):
        return self.in_loop or 0 <= self.base - lag < B

    def parity(self, lag):
        return (self.base - lag) % 2

    def half(self, lag):
        return self.i + (self.base - lag) // 2 if self.in_loop else (self.base - lag) // 2


def run_steps(eng, body):
    for s in range(-1, PEELED_FIRST):
        body(Step(s))
    with eng.Fori(0, (B - 2 - PEELED_FIRST) // UNROLL) as i:
        for k in range(UNROLL):
            body(Step(PEELED_FIRST + k, i, True))
    for s in range(B - 2, B + 2):
        body(Step(s))


def wait_count(eng, sem, value):
    if not isinstance(value, int) or value > 0:
        eng.wait_ge(sem, value)


def wait_apart(eng, sem, value, passed):
    eng.wait_ge(sem, value)
    eng.sem_inc(passed, 1)


def build(nc, x, ctx, mask, wq, bq, wk, bk, wv, bv, wo, bo, rms_w, gate_w, w1, b1, w2, b2, out):
    sorted_rows = nc.dram_tensor("sorted_rows", [FFN_TILES * P, ROW], F32).ap()
    w2_spill = nc.dram_tensor("w2_spill", [P, 2, B, W_CHUNK], F16).ap()
    x1_rows = nc.dram_tensor("x1_rows", [B, T, D], F32).ap()
    q_spill = [nc.dram_tensor(f"q_spill{i}", [2, P, DT * 2 * T], F16).ap() for i in range(2)]
    k_spill = [nc.dram_tensor(f"k_spill{i}", [2, P, DT * S], F16).ap() for i in range(2)]

    with ExitStack() as stack:
        def sb(name, shape, dt=F32):
            return stack.enter_context(nc.sbuf_tensor(name, shape, dt))

        def sem(name):
            return stack.enter_context(nc.semaphore(name))

        arena_a = sb("arena_a", [P, EXPERTS * FT * D])
        arena_b = sb("arena_b", [P, 10752])
        used = {"a": 0, "b": 0}

        def carve(which, parts, *shape):
            arena = arena_a if which == "a" else arena_b
            n = 1
            for d in shape:
                n *= d
            at = used[which]
            used[which] += n + n % 2
            assert used[which] <= arena.shape[1]
            flat = arena[0:parts, at:at + n]
            if len(shape) == 1:
                return flat
            names = "abcd"[:len(shape)]
            return flat.rearrange(f"p ({' '.join(names)}) -> p {' '.join(names)}",
                                  **{k: v for k, v in zip(names, shape)})

        ident = sb("ident", [P, P])
        w1_parts = sb("w1_parts", [P, 2, EXPERTS, DT, F], F16)
        b1_sb = sb("b1_sb", [P, EXPERTS, FT])
        xr_all = sb("xr_all", [T, B, ROW])
        gate_logits = sb("gate_logits", [T, B, EXPERTS])
        slot_of = sb("slot_of", [T, B], U32)
        tile_expert = sb("tile_expert", [1, FFN_TILES + 1], I32)

        wq_sb = carve("a", P, DT, D)
        wk_parts = carve("a", P, DT * D).bitcast(F16).rearrange("p (s t d) -> p s t d", s=2, t=DT)
        wv_parts = carve("a", P, DT * D).bitcast(F16).rearrange("p (s t d) -> p s t d", s=2, t=DT)
        wo_sb = carve("a", P, DT, D)
        gw_sb = carve("a", P, DT, EXPERTS)
        gw_rows = carve("a", EXPERTS, D)
        bq_sb = carve("a", P, DT)
        bk_sb = carve("a", P, DT)
        bv_cols = carve("a", P, DT)
        bv_rep = carve("a", P, DT, T)
        bvo = carve("a", T, D)
        rmsw = carve("a", T, D)
        mask_bias = carve("a", T, S)
        pair_rows = carve("a", P, 2)
        eps_ln = carve("a", T, 1)
        eps_rms = carve("a", T, 1)
        minus_half = carve("a", T, 1)
        x_in = [carve("a", T, D) for _ in range(2)]
        x_res = [carve("a", T, D) for _ in range(2)]
        xn = carve("a", T, D)
        xnT = carve("a", P, DT, T)
        q1 = carve("a", P, DT, T)
        q_masked = carve("a", P, DT, 2, T)
        q_parts = carve("a", P, 2 * DT * T).bitcast(F16).rearrange("p (s j a t) -> p s j a t", s=2, j=DT, a=2)
        k_parts = carve("a", P, DT * S).bitcast(F16).rearrange("p (s j k) -> p s j k", s=2, j=DT)
        q_stack_words = [carve("a", P, PAIRS * DT * T) for _ in range(2)]
        q_stack = [words.bitcast(F16).rearrange("p (r j a t) -> p r j a t", r=PAIRS, j=DT, a=2)
                   for words in q_stack_words]
        ctx_in = [carve("b", CK, CHUNKS, D) for _ in range(2)]
        ctx_parts = [carve("b", P, DT * S).bitcast(F16).rearrange("p (s j k) -> p s j k", s=2, j=DT)
                     for _ in range(2)]
        k_stack_words = [carve("a", P, PAIRS * DT * S // 2) for _ in range(2)]
        k_stack = [words.bitcast(F16).rearrange("p (r j k) -> p r j k", r=PAIRS, j=DT) for words in k_stack_words]
        wv_in = q_stack_words[0][:, 0:DT * D].rearrange("p (t d) -> p t d", t=DT)
        wq_in, wk_in = [words[:, 0:DT * D].rearrange("p (t d) -> p t d", t=DT) for words in k_stack_words]
        v_aug = [carve("b", CK, CHUNKS, H, VW) for _ in range(2)]
        probs = [carve("a", T, S) for _ in range(4)]
        probsT = [carve("a", CK, CHUNKS, T) for _ in range(8)]
        minus_max = carve("a", T, 4)
        oT = carve("b", P, 4, T)
        rden = carve("a", T, H)
        att = carve("b", T, D)
        attT = carve("b", P, DT, T)
        x1 = [carve("b", T, D) for _ in range(2)]
        centred = carve("b", T, D)
        xr_now = carve("b", T, D)
        xrT = carve("b", P, DT, T)
        st1 = carve("b", T, 6)
        mv1 = carve("b", T, 2)
        var1 = carve("b", T, 1)
        rstd = carve("b", T, 1)
        st2 = carve("b", T, 6)
        mv2 = carve("b", T, 2)
        ln2 = carve("b", T, 8)
        zeros = carve("b", P, ROW)
        token_i = carve("b", T, B).bitcast(I32)
        b1_rows = carve("b", EXPERTS * FT, P)
        w_scale = carve("b", P, 1)
        w_in = [[carve("b", P, W_CHUNK) for _ in range(2)] for _ in range(2)]
        w_scaled = carve("b", P, W_CHUNK)
        w2_split = carve("b", P, W_CHUNK).bitcast(F16).rearrange("p (s n) -> p s n", s=2)

        w2_parts = arena_a[:, :].bitcast(F16).rearrange("p (s e f d) -> p s e f d", s=2, e=EXPERTS, f=FT)
        used["b"] = 0
        xs = [carve("b", P, ROW) for _ in range(FFN_UNROLL)]
        token_of = [carve("b", P, 1).bitcast(U32) for _ in range(FFN_UNROLL)]
        x1_got = [carve("b", P, D) for _ in range(FFN_UNROLL)]
        x_parts = [carve("b", P, DT * P).bitcast(F16).rearrange("p (s j t) -> p s j t", s=2, j=DT) for _ in range(2)]
        b2_rep = [carve("b", P, D) for _ in range(2)]
        h_act = carve("b", P, FT, P)
        h_parts = [carve("b", P, FT * P).bitcast(F16).rearrange("p (s f t) -> p s f t", s=2, f=FT) for _ in range(2)]
        y_sb = carve("b", P, D)
        out_rows = [carve("b", P, D) for _ in range(FFN_UNROLL)]
        used["b"] = 0
        small = [carve("b", P, B, EXPERTS) for _ in range(9)]
        small_te = carve("b", P, EXPERTS, B)
        small_e = carve("b", P, 12, EXPERTS)
        small_b = carve("b", P, 6, B)
        iota_i = carve("b", P, B * EXPERTS).bitcast(I32)
        upper = carve("b", P, P)
        ones = carve("b", P, P)
        tile_no = carve("b", 1, FFN_TILES, EXPERTS)
        tile_cmp = carve("b", 1, FFN_TILES, EXPERTS)
        tile_sum = carve("b", 1, FFN_TILES)
        ps = stack.enter_context(nc.psum_tensor("ps", [P, 8, 512], F32))
        score_bank = [ps[:, 0, :], ps[:, 1, :]]
        probT_bank = [ps[:, 2, :], ps[:, 3, :]]
        out_bank = ps[:, 4, :]
        proj_bank = [ps[:, 5, :], ps[:, 6, :]]
        tail_bank = ps[:, 7, :]

        constants = sem("constants")
        const_dve = sem("const_dve")
        mask_ready = sem("mask_ready")
        weights_loaded = sem("weights_loaded")
        setup_pe = sem("setup_pe")
        setup_copied = sem("setup_copied")
        ctx_loaded = [sem("ctx_loaded0"), sem("ctx_loaded1")]
        x_loaded = [sem("x_loaded0"), sem("x_loaded1")]
        ln1_stats = sem("ln1_stats")
        ln1_mean = sem("ln1_mean")
        ln1_var = sem("ln1_var")
        rstd_ready = sem("rstd_ready")
        xn_ready = sem("xn_ready")
        res_ready = sem("res_ready")
        proj_ready = sem("proj_ready")
        proj_copied = [sem("proj_copied0"), sem("proj_copied1")]
        q1_ready = sem("q1_ready")
        q_masked_ready = sem("q_masked_ready")
        q_parts_ready = sem("q_parts_ready")
        k_high_ready = sem("k_high_ready")
        ctx_high_ready = sem("ctx_high_ready")
        weights_high_ready = sem("weights_high_ready")
        q_spilled = sem("q_spilled")
        k_spilled = sem("k_spilled")
        q_stacked = [sem("q_stacked0"), sem("q_stacked1")]
        k_stacked = [sem("k_stacked0"), sem("k_stacked1")]
        scores_ready = sem("scores_ready")
        max_ready = sem("max_ready")
        probs_ready = sem("probs_ready")
        probsT_ready = sem("probsT_ready")
        probsT_copied = [sem("probsT_copied_act"), sem("probsT_copied_dve")]
        pv_done = sem("pv_done")
        out_copied = sem("out_copied")
        rden_ready = sem("rden_ready")
        tail_ready = sem("tail_ready")
        tail_copied = sem("tail_copied")
        x1_spilled = [sem("x1_spilled0"), sem("x1_spilled1")]
        ln2_stats = sem("ln2_stats")
        ln2_mean = sem("ln2_mean")
        ln2_chain = sem("ln2_chain")
        centred_ready = sem("centred_ready")
        xr_ready = sem("xr_ready")
        zeroed = sem("zeroed")
        w_staged = [sem("w_staged0"), sem("w_staged1")]
        w1_scaled = sem("w1_scaled")
        w1_split = sem("w1_split")
        w2_scaled = sem("w2_scaled")
        w2_split_ready = sem("w2_split_ready")
        w2_spilled = sem("w2_spilled")
        w2_loaded = sem("w2_loaded")
        route = sem("route")
        route_iota = sem("route_iota")
        route_exp = sem("route_exp")
        ranks_ready = sem("ranks_ready")
        scattered = sem("scattered")
        xs_loaded = [sem(f"xs_loaded{i}") for i in range(FFN_UNROLL)]
        b2_loaded = [sem("b2_loaded0"), sem("b2_loaded1")]
        xsT_ready = sem("xsT_ready")
        x_high_ready = sem("x_high_ready")
        x_low_ready = sem("x_low_ready")
        h_ready = sem("h_ready")
        h_activated = sem("h_activated")
        h_high_ready = sem("h_high_ready")
        h_low_ready = sem("h_low_ready")
        y_ready = sem("y_ready")
        y_biased = sem("y_biased")
        token_ready = sem("token_ready")
        x1_got_clear = sem("x1_got_clear")
        x1_gathered = [sem(f"x1_gathered{i}") for i in range(FFN_UNROLL)]
        out_ready = sem("out_ready")
        out_stored = [sem(f"out_stored{i}") for i in range(FFN_UNROLL)]
        tokens_numbered = sem("tokens_numbered")

        dve_passed = sem("dve_passed")
        sp_passed = sem("sp_passed")
        pool_passed = sem("pool_passed")

        block = stack.enter_context(nc.Block())

        N_WEIGHTS = 10 + 2 * PAIRS
        Q_MOVED, K_MOVED = 16 * 2, 16 * len(GROUPS)
        N_CONST_POOL = 3
        N_CONST_DVE = 13 + DT * DT

        @block.sync
        def _(sp):
            def load_batch(b, parity):
                sp.dma_start(ctx_in[parity], ctx[bass.ds(b, 1)].rearrange(
                    "o (c k) d -> k (o c) d", c=CHUNKS)).then_inc(ctx_loaded[parity], 16)
                sp.dma_start(x_in[parity], x[bass.ds(b, 1)].rearrange(
                    "o t d -> t (o d)")).then_inc(x_loaded[parity], 16)

            load_batch(0, 0)
            for dst, src in ((wk_in, wk), (wv_in, wv), (wq_in, wq), (wo_sb, wo)):
                sp.dma_start(dst, src.rearrange("(t p) n -> p t n", p=P)).then_inc(weights_loaded, 16)
            sp.dma_start(bv_cols, bv.rearrange("(t p) -> p t", p=P),
                         allow_slow_non_contiguous=True).then_inc(weights_loaded, 16)
            sp.dma_start(mask_bias, mask.rearrange("a b t s -> (a b t) s")).then_inc(weights_loaded, 16)
            sp.dma_start(bvo, bo.partition_broadcast(T)).then_inc(weights_loaded, 16)
            sp.dma_start(rmsw, rms_w.partition_broadcast(T)).then_inc(weights_loaded, 16)
            sp.dma_start(gw_rows, gate_w).then_inc(weights_loaded, 16)
            sp.dma_start(b1_rows, b1.rearrange("e (f p) -> (e f) p", p=P)).then_inc(weights_loaded, 16)
            load_batch(1, 1)
            sp.wait_ge(constants, N_CONST_POOL)
            sp.dma_start(sorted_rows.rearrange("(n p) d -> p n d", p=P),
                         zeros.unsqueeze(1).to_broadcast([P, FFN_TILES, ROW])).then_inc(zeroed, 16)

            def step(st):
                if st.exists(0) and st.exists(-2):
                    wait_apart(sp, proj_ready, 8 * st.batch(0) + 2, sp_passed)
                    wait_apart(sp, res_ready, st.batch(0) + 1, sp_passed)
                    load_batch(st.batch(-2), st.parity(-2))
                if st.exists(1):
                    sp.wait_ge(w2_split_ready, st.batch(1) + 1)
                    sp.dma_start(w2_spill[:, :, bass.ds(st.batch(1), 1), :].rearrange("p s o n -> p s (o n)"),
                                 w2_split).then_inc(w2_spilled, 16)
                if st.exists(-1):
                    b, par = st.batch(-1), st.parity(-1)
                    wait_count(sp, w2_split_ready, b - 1 if st.in_loop or b > 1 else 0)
                    cols = slice(par * W_CHUNK, (par + 1) * W_CHUNK)
                    sp.dma_start(w_in[0][par], w1.rearrange("e (t p) f -> (e t) p f", p=P)[
                        bass.ds(st.half(-1), 1), :, cols].rearrange("o p f -> p (o f)")).then_inc(w_staged[par], 16)
                    sp.dma_start(w_in[1][par].rearrange("p (f d) -> p f d", d=D),
                                 w2.rearrange("e (f p) d -> (e f) p d", p=P)[
                        bass.ds(b * (W_CHUNK // D), W_CHUNK // D)].rearrange("f p d -> p f d")
                                 ).then_inc(w_staged[par], 16)
                    wait_count(sp, scores_ready, H * (b - 1) if st.in_loop or b >= 2 else 0)
                    sp.wait_ge(proj_copied[0], 4 * b + 2)
                    wait_apart(sp, proj_copied[1], 4 * b + 2, sp_passed)
                    sp.dma_start(k_spill[par].rearrange("s p n -> p s n"),
                                 k_parts.rearrange("p s j k -> p s (j k)")).then_inc(k_spilled, 16)
                    sp.wait_ge(k_spilled, 16 * (b + 1))
                    for g, (part, _) in enumerate(GROUPS):
                        sp.dma_start(k_stack[par][32 * g:32 * g + 32].rearrange("p r j k -> p (r j k)"),
                                     k_spill[par][part].rearrange("(i r) n -> i (r n)", r=PAIRS)
                                     ).then_inc(k_stacked[par], 16)
                    wait_apart(sp, q_parts_ready, b + 1, sp_passed)
                    sp.dma_start(q_spill[par].rearrange("s p n -> p s n"),
                                 q_parts.rearrange("p s j a t -> p s (j a t)")).then_inc(q_spilled, 16)
                    sp.wait_ge(q_spilled, 16 * (b + 1))
                    for g in (0, 2):
                        sp.dma_start(q_stack[par][32 * g:32 * g + 64].rearrange("p r j a t -> p (r j a t)"),
                                     q_spill[par].rearrange("s (i r) n -> (s i) (r n)", r=PAIRS)
                                     ).then_inc(q_stacked[par], 16)
                if st.exists(1):
                    sp.wait_ge(tail_copied, 5 * st.batch(1) + 3)
                    sp.dma_start(x1_rows[bass.ds(st.batch(1), 1)].rearrange("o t d -> t (o d)"),
                                 x1[st.parity(1)]).then_inc(x1_spilled[st.parity(1)], 16)

            run_steps(sp, step)

            sp.wait_ge(tail_copied, 5 * B)
            sp.wait_ge(xr_ready, 2 * B)
            sp.wait_ge(x1_spilled[0], 16 * B // 2)
            sp.wait_ge(x1_spilled[1], 16 * B // 2)
            sp.wait_ge(w2_spilled, 16 * B)
            for part in range(2):
                for q in range(4):
                    sp.dma_start(w2_parts[:, part, 2 * q:2 * q + 2].rearrange("p e f d -> p (e f d)"),
                                 w2_spill[:, part, B // 4 * q:B // 4 * (q + 1)].rearrange("p b n -> p (b n)")
                                 ).then_inc(w2_loaded, 16)
            sp.wait_ge(scattered, 16 * B)

            def load_rows(t, buffer):
                sp.dma_start(xs[buffer], sorted_rows[bass.ds(t * P, P), :]).then_inc(xs_loaded[buffer], 16)

            def load_b2(t, parity):
                e = sp.value_load(tile_expert[0:1, bass.ds(t, 1)], min_val=0, max_val=EXPERTS - 1)
                sp.dma_start(b2_rep[parity], b2[bass.ds(e, 1), :].rearrange("o f -> (o f)").partition_broadcast(P)
                             ).then_inc(b2_loaded[parity], 16)

            def next_loads(t, buffer, rows, bias):
                if rows:
                    wait_apart(sp, out_ready, t + 1, sp_passed)
                    load_rows(t + FFN_UNROLL, buffer)
                if bias:
                    wait_apart(sp, y_biased, t + 1, sp_passed)
                    load_b2(t + 2, buffer % 2)

            for t in range(FFN_UNROLL):
                load_rows(t, t)
                if t < 2:
                    load_b2(t, t)
            with sp.Fori(0, FFN_LOOPS) as i:
                for k in range(FFN_UNROLL):
                    next_loads(FFN_UNROLL * i + k, k, True, True)
            for t in range(FFN_UNROLL * FFN_LOOPS, FFN_TILES - 2):
                next_loads(t, t % FFN_UNROLL, t + FFN_UNROLL < FFN_TILES, True)
            for i in range(FFN_UNROLL):
                sp.wait_ge(out_stored[i], 16 * len(range(i, FFN_TILES, FFN_UNROLL)))

        @block.gpsimd
        def _(pool):
            pool.memset(ident[:, :], 0.0).then_inc(constants, 1)
            pool.memset(zeros, 0.0).then_inc(constants, 1)
            pool.wait_ge(constants, 2)
            pool.affine_select(out=ident[:, :], in_=ident[:, :], compare_op=ALU.not_equal, fill=1.0,
                               base=0, pattern=[[-1, P]], channel_multiplier=1).then_inc(constants, 1)
            pool.wait_ge(constants, N_CONST_POOL)
            pool.wait_ge(const_dve, N_CONST_DVE)

            def queries_rstd(b):
                wait_count(pool, xn_ready, b)
                pool.wait_ge(ln1_mean, b + 1)
                pool.tensor_tensor(var1, mv1[:, 1:2], eps_ln, ALU.add).then_inc(ln1_var, 1)
                pool.wait_ge(ln1_var, b + 1)
                pool.tensor_tensor(rstd, var1, minus_half, ALU.pow).then_inc(rstd_ready, 1)

            def step(st):
                if st.exists(2):
                    b = st.batch(2)
                    wait_count(pool, tail_copied, 5 * b)
                    pool.wait_ge(centred_ready, b + 1)
                    pool.tensor_tensor(xr_now, centred, rmsw, ALU.mult).then_inc(xr_ready, 1)
                    pool.tensor_tensor(xr_all[:, bass.ds(b, 1), 0:D].rearrange("p o d -> p (o d)"),
                                       centred, rmsw, ALU.mult).then_inc(xr_ready, 1)
                if st.exists(-1):
                    b, par = st.batch(-1), st.parity(-1)
                    pool.wait_ge(q1_ready, b + 1)
                    pool.wait_ge(proj_copied[1], 4 * b + 3)
                    if st.exists(0):
                        pool.wait_ge(q_spilled, 16 * b)
                    q_both = q1.unsqueeze(2).to_broadcast([P, DT, 2, T])
                    rows = pair_rows.unsqueeze(1).unsqueeze(3).to_broadcast([P, DT, 2, T])
                    pool.tensor_tensor(q_masked, q_both, rows, ALU.mult).then_inc(q_masked_ready, 1)
                    pool.tensor_tensor(q_parts[:, 0], q_both, rows, ALU.mult).then_inc(q_masked_ready, 1)
                    pool.wait_ge(q_masked_ready, 2 * (b + 1))
                    pool.tensor_tensor(q_parts[:, 1], q_masked, q_parts[:, 0], ALU.subtract).then_inc(q_parts_ready, 1)
                if st.exists(0):
                    b, par = st.batch(0), st.parity(0)
                    scale = w_scale.to_broadcast([P, W_CHUNK])
                    w1_chunk = [w1_parts[:, part].rearrange("p e t f -> p (e t f)")[:, bass.ds(b * W_CHUNK, W_CHUNK)]
                                for part in range(2)]
                    pool.wait_ge(w_staged[par], 32 * (st.half(0) + 1))
                    wait_count(pool, w2_split_ready, b)
                    pool.tensor_tensor(w_scaled, w_in[0][par], scale, ALU.mult).then_inc(w1_scaled, 1)
                    pool.tensor_tensor(w1_chunk[0], w_in[0][par], scale, ALU.mult).then_inc(w1_scaled, 1)
                    pool.wait_ge(w1_scaled, 2 * (b + 1))
                    pool.tensor_tensor(w1_chunk[1], w_scaled, w1_chunk[0], ALU.subtract).then_inc(w1_split, 1)
                    pool.wait_ge(w1_split, b + 1)
                    wait_count(pool, w2_spilled, 16 * b)
                    pool.tensor_tensor(w_scaled, w_in[1][par], scale, ALU.mult).then_inc(w2_scaled, 1)
                    pool.tensor_tensor(w2_split[:, 0, :], w_in[1][par], scale, ALU.mult).then_inc(w2_scaled, 1)
                    pool.wait_ge(w2_scaled, 2 * (b + 1))
                    pool.tensor_tensor(w2_split[:, 1, :], w_scaled, w2_split[:, 0, :], ALU.subtract
                                       ).then_inc(w2_split_ready, 1)
                if st.exists(-2):
                    queries_rstd(st.batch(-2))
                if st.exists(1):
                    b = st.batch(1)
                    c = 7 * b
                    wait_count(pool, centred_ready, b)
                    pool.wait_ge(ln2_mean, b + 1)
                    for k, a0, a1, op in ((0, mv2[:, 1:2], eps_ln, ALU.add),
                                          (1, ln2[:, 0:1], minus_half, ALU.pow),
                                          (2, mv2[:, 1:2], ln2[:, 1:2], ALU.mult),
                                          (3, ln2[:, 2:3], ln2[:, 1:2], ALU.mult),
                                          (4, ln2[:, 3:4], eps_rms, ALU.add),
                                          (5, ln2[:, 4:5], minus_half, ALU.pow),
                                          (6, ln2[:, 5:6], ln2[:, 1:2], ALU.mult)):
                        pool.tensor_tensor(ln2[:, k:k + 1], a0, a1, op).then_inc(ln2_chain, 1)
                        pool.wait_ge(ln2_chain, c + k + 1)
                if st.exists(-1):
                    b, par = st.batch(-1), st.parity(-1)
                    if st.exists(1):
                        pool.wait_ge(tail_copied, 5 * st.batch(1) + 3)
                    pool.wait_ge(xn_ready, b + 1)
                    pool.tensor_tensor(x_res[par], x_in[par], bvo, ALU.add).then_inc(res_ready, 1)

            pool.wait_ge(setup_copied, 3)
            pool.iota(token_i, pattern=[[-T, B]], base=NO_TOKEN, channel_multiplier=-1).then_inc(tokens_numbered, 1)
            pool.wait_ge(tokens_numbered, 1)
            pool.tensor_copy(xr_all[:, :, D + 1], token_i).then_inc(tokens_numbered, 1)
            queries_rstd(0)
            run_steps(pool, step)

            pool.wait_ge(tail_copied, 5 * B)
            pool.wait_ge(xr_ready, 2 * B)
            pool.wait_ge(zeroed, 16)
            pool.iota(iota_i.rearrange("p (b e) -> p b e", b=B), pattern=[[0, B], [-1, EXPERTS]], base=EXPERTS,
                      channel_multiplier=0).then_inc(route_iota, 1)
            pool.wait_ge(route_iota, 1)
            pool.tensor_copy(small[0], iota_i.rearrange("p (b e) -> p b e", b=B)).then_inc(route_iota, 1)
            pool.wait_ge(route_iota, 2)
            pool.iota(iota_i.rearrange("p (e j) -> p e j", e=EXPERTS), pattern=[[0, EXPERTS], [P, B]], base=0,
                      channel_multiplier=0).then_inc(route_iota, 1)
            pool.wait_ge(route_iota, 3)
            pool.tensor_copy(small_te, iota_i.rearrange("p (e j) -> p e j", e=EXPERTS)).then_inc(route_iota, 1)
            pool.memset(upper, 1.0).then_inc(route_iota, 1)
            pool.memset(ones, 1.0).then_inc(route_iota, 1)
            pool.wait_ge(route_iota, 6)
            pool.affine_select(out=upper, in_=upper, compare_op=ALU.is_gt, fill=0.0,
                               base=0, pattern=[[1, P]], channel_multiplier=-1).then_inc(route_iota, 1)
            pool.iota(iota_i[0:1, 0:B * EXPERTS].rearrange("p (t e) -> p t e", e=EXPERTS),
                      pattern=[[1, B], [0, EXPERTS]], base=0, channel_multiplier=0).then_inc(route_iota, 1)
            pool.wait_ge(route_iota, 8)
            pool.tensor_copy(tile_no[:, 0:B, :],
                             iota_i[0:1, 0:B * EXPERTS].rearrange("p (t e) -> p t e", e=EXPERTS)).then_inc(route_iota, 1)
            pool.wait_ge(route_iota, 9)
            left = FFN_TILES - B
            pool.iota(iota_i[0:1, 0:left * EXPERTS].rearrange("p (t e) -> p t e", e=EXPERTS),
                      pattern=[[1, left], [0, EXPERTS]], base=B, channel_multiplier=0).then_inc(route_iota, 1)
            pool.wait_ge(route_iota, 10)
            pool.tensor_copy(tile_no[:, B:FFN_TILES, :],
                             iota_i[0:1, 0:left * EXPERTS].rearrange("p (t e) -> p t e", e=EXPERTS)
                             ).then_inc(route_iota, 1)
            pool.wait_ge(route, N_ROUTE)
            for b in range(B):
                pool.indirect_dma_start(out=sorted_rows, out_offset=bass.IndirectOffsetOnAxis(ap=slot_of[:, b:b + 1], axis=0),
                                        in_=xr_all[:, b, :], in_offset=None).then_inc(scattered, 16)
            for i in range(FFN_UNROLL):
                pool.wait_ge(scattered, 16 * B)
                pool.memset(x1_got[i], 0.0).then_inc(x1_got_clear, 1)
            pool.wait_ge(x1_got_clear, FFN_UNROLL)

            def gather(t, buffer, first):
                if not first:
                    pool.wait_ge(out_ready, t + 1 - FFN_UNROLL)
                wait_apart(pool, token_ready, t + 1, pool_passed)
                pool.indirect_dma_start(out=x1_got[buffer], out_offset=None, in_=x1_rows.rearrange("b t d -> (b t) d"),
                                        in_offset=bass.IndirectOffsetOnAxis(ap=token_of[buffer], axis=0),
                                        bounds_check=B * T - 1, oob_is_err=False).then_inc(x1_gathered[buffer], 16)

            def scatter(t, buffer):
                wait_apart(pool, out_ready, t + 1, pool_passed)
                pool.indirect_dma_start(out=out.rearrange("b t d -> (b t) d"),
                                        out_offset=bass.IndirectOffsetOnAxis(ap=token_of[buffer], axis=0),
                                        in_=out_rows[buffer], in_offset=None,
                                        bounds_check=B * T - 1, oob_is_err=False).then_inc(out_stored[buffer], 16)

            for t in range(FFN_PEELED):
                gather(t, t, True)
            scatter(0, 0)
            gather(3, 3, True)
            scatter(1, 1)
            with pool.Fori(0, FFN_LOOPS) as i:
                for k in range(FFN_UNROLL):
                    t = FFN_UNROLL * i + FFN_PEELED + 1 + k
                    gather(t, k, False)
                    scatter(t - 2, (k + 2) % FFN_UNROLL)
            for t in range(FFN_TILES - 3, FFN_TILES):
                if t >= FFN_PEELED + 1 + FFN_UNROLL * FFN_LOOPS:
                    gather(t, t % FFN_UNROLL, False)
                    scatter(t - 2, (t - 2) % FFN_UNROLL)
            for t in range(FFN_TILES - 2, FFN_TILES):
                scatter(t, t % FFN_UNROLL)

        @block.scalar
        def _(act):
            for dst, src in ((bk_sb, bk), (bq_sb, bq)):
                for r in range(PAIRS):
                    act.dma_start(dst[r:P:PAIRS], src.rearrange("(j r i) -> r i j", r=PAIRS, i=32)[r],
                                  allow_slow_non_contiguous=True).then_inc(weights_loaded, 16)
            act.wait_ge(setup_pe, 1)
            nc.scalar.activation(gw_sb, tail_bank[:, 0:DT * EXPERTS].rearrange("p (t e) -> p t e", t=DT),
                                 ACT.Copy).then_inc(setup_copied, 1)
            nc.scalar.activation(b1_sb[:, :, :].rearrange("p e f -> p (e f)"),
                                 tail_bank[:, DT * EXPERTS:DT * EXPERTS + EXPERTS * FT], ACT.Copy
                                 ).then_inc(setup_copied, 1)

            def copy_probsT(lag, head):
                act.wait_ge(probsT_ready, H * st_.batch(lag) + head + 1)
                slot_free(act, lag, head)
                nc.scalar.activation(probsT[head % 8], probT_bank[head % 2][0:CK, 0:CHUNKS * T].rearrange(
                    "p (c t) -> p c t", c=CHUNKS), ACT.Copy).then_inc(probsT_copied[0], 1)

            def slot_free(eng, lag, head):
                quads = 4 * st_.batch(lag) + head // 4 - 1
                wait_count(eng, pv_done, quads)

            def context_high(b, par, j):
                act.wait_ge(proj_ready, 8 * b + 1 + j)
                nc.scalar.activation(ctx_parts[par][:, 0, j, :], proj_bank[j][:, 0:S], ACT.Copy
                                     ).then_inc(ctx_high_ready, 1)

            def copy_values(b, par, j):
                act.wait_ge(proj_ready, 8 * b + 7 + j)
                wait_count(act, pv_done, 4 * (b - 1))
                n = 2 - j
                nc.scalar.activation(v_aug[par][:, 2 * j:2 * j + n, :, 0:DH],
                                     proj_bank[j][0:CK, 0:n * D].rearrange("p (c h d) -> p c h d", c=n, h=H),
                                     ACT.Copy, scale=1.0 / SCALE_V).then_inc(proj_copied[j], 1)

            def step(st):
                nonlocal st_
                st_ = st
                for slot in range(H):
                    lag, head = (0, slot - HEAD_LAG_COPY) if slot >= HEAD_LAG_COPY else (1, H + slot - HEAD_LAG_COPY)
                    if head % 2 == 0 and st.exists(lag):
                        copy_probsT(lag, head)
                    if st.exists(-2) and slot - 1 in CONTEXT_SLOTS:
                        context_high(st.batch(-2), st.parity(-2), CONTEXT_SLOTS.index(slot - 1))
                    if st.exists(-1):
                        b, par = st.batch(-1), st.parity(-1)
                        if slot - 1 in VALUES_SLOTS[1:]:
                            copy_values(b, par, VALUES_SLOTS.index(slot - 1) - 1)
                        if slot in (1, 4):
                            j = slot // 4
                            act.wait_ge(proj_ready, 8 * b + 3 + j)
                            if st.exists(0):
                                act.wait_ge(k_spilled, 16 * b)
                            nc.scalar.activation(k_parts[:, 0, j, :], proj_bank[j][:, 0:S], ACT.Identity,
                                                 bias=bk_sb[:, j:j + 1]).then_inc(k_high_ready, 1)
                        if slot == 5:
                            act.wait_ge(proj_ready, 8 * b + 5)
                            nc.scalar.activation(xnT, proj_bank[0][:, 0:DT * T].rearrange("p (j t) -> p j t", j=DT),
                                                 ACT.Copy).then_inc(proj_copied[0], 1)
                    if st.exists(1):
                        b = st.batch(1)
                        if slot == 6:
                            act.wait_ge(pv_done, 4 * b + 4)
                            wait_count(act, tail_ready, 5 * b - 4 if st.in_loop or b >= 1 else 0)
                            nc.scalar.activation(oT, out_bank[:, 0:4 * T].rearrange("p (g t) -> p g t", g=4),
                                                 ACT.Copy).then_inc(out_copied, 1)
                        if slot == 13:
                            act.wait_ge(tail_ready, 5 * b + 2)
                            nc.scalar.activation(attT, tail_bank[:, 0:DT * T].rearrange("p (j t) -> p j t", j=DT),
                                                 ACT.Copy).then_inc(tail_copied, 1)
                    if st.exists(2) and slot == 6:
                        act.wait_ge(tail_ready, 5 * st.batch(2) + 4)
                        nc.scalar.activation(xrT, tail_bank[:, 0:DT * T].rearrange("p (j t) -> p j t", j=DT),
                                             ACT.Copy).then_inc(tail_copied, 1)
                    if st.exists(0):
                        act.wait_ge(max_ready, H * st.batch(0) + slot + 1)
                        nc.scalar.activation(probs[slot % 4], probs[slot % 4], ACT.Exp,
                                             bias=minus_max[:, slot % 4:slot % 4 + 1], scale=-1.0
                                             ).then_inc(probs_ready, 1)

            st_ = None
            for j in range(DT):
                context_high(0, 0, j)
            run_steps(act, step)
            act.wait_ge(route, R_DIFF)
            nc.scalar.activation(small[2][0:T], small[1][0:T], ACT.Exp).then_inc(route_exp, 1)

            def rows_high(t, parity, first):
                act.wait_ge(xsT_ready, t + 1)
                if not first:
                    act.wait_ge(h_ready, 2 * t - 2)
                nc.scalar.activation(x_parts[parity][:, 0], ps[:, 0, 0:DT * P].rearrange("p (j t) -> p j t", j=DT),
                                     ACT.Copy, scale=SCALE_X).then_inc(x_high_ready, 1)

            def activate(t, parity, first):
                e = act.value_load(tile_expert[0:1, bass.ds(t, 1)], min_val=0, max_val=EXPERTS - 1)
                for half in range(2):
                    act.wait_ge(h_ready, 2 * t + 1 + half)
                    if not first:
                        act.wait_ge(h_low_ready, 2 * t - 1 + half)
                    for f in range(FT // 2 * half, FT // 2 * (half + 1)):
                        last = nc.scalar.activation(
                            h_act[:, f, :], ps[:, 1 + 2 * parity + f // 4, (f % 4) * P:(f % 4 + 1) * P], ACT.Silu,
                            bias=b1_sb[:, bass.ds(e, 1), f], scale=1.0 / (SCALE_W * SCALE_X))
                    last.then_inc(h_activated, 1)

            act.wait_ge(scattered, 16 * B)
            rows_high(0, 0, True)
            rows_high(1, 1, True)
            activate(0, 0, True)
            rows_high(2, 0, False)
            activate(1, 1, False)
            rows_high(3, 1, False)
            activate(2, 0, False)
            with act.Fori(0, FFN_LOOPS) as i:
                for k in range(FFN_UNROLL):
                    t = FFN_UNROLL * i + FFN_PEELED + k
                    rows_high(t + 1, k % 2, False)
                    activate(t, (1 + k) % 2, False)
            for t in range(FFN_PEELED + FFN_UNROLL * FFN_LOOPS, FFN_TILES):
                if t + 1 < FFN_TILES:
                    rows_high(t + 1, (t + 1) % 2, False)
                activate(t, t % 2, False)

        @block.tensor
        def _(pe):
            pe.wait_ge(constants, N_CONST_POOL)
            pe.wait_ge(weights_loaded, 16 * N_WEIGHTS)
            for j in range(DT):
                mm = pe.transpose(tail_bank[:, j * EXPERTS:(j + 1) * EXPERTS], gw_rows[:, j * P:(j + 1) * P],
                                  ident[0:EXPERTS, 0:EXPERTS])
            mm = pe.transpose(tail_bank[:, DT * EXPERTS:DT * EXPERTS + EXPERTS * FT], b1_rows,
                              ident[0:EXPERTS * FT, 0:EXPERTS * FT])
            mm.then_inc(setup_pe, 1)
            pe.wait_ge(const_dve, N_CONST_DVE)
            for j in range(DT):
                mm = pe.matmul(proj_bank[0][0:T, 0:D], bv_rep[:, j, :], wo_sb[:, j, :], start=j == 0, stop=j == DT - 1)
            mm.then_inc(setup_pe, 1)
            pe.wait_ge(setup_copied, 3)

            def scores(st, head):
                b = st.batch(0)
                if head == 0:
                    pe.wait_ge(q_stacked[st.parity(0)], Q_MOVED * (st.half(0) + 1))
                    pe.wait_ge(k_stacked[st.parity(0)], K_MOVED * (st.half(0) + 1))
                wait_count(pe, max_ready, H * b + head - 1)
                j, r, a = head // HPT, head % HPT // 2, head % 2
                pe.matmul(score_bank[head % 2][0:T, 0:S], q_stack[st.parity(0)][:, r, j, a, :],
                          k_stack[st.parity(0)][:, r, j, :], start=True, stop=True).then_inc(scores_ready, 1)

            def transpose_probs(st, lag, head):
                b = st.batch(lag)
                wait_count(pe, probsT_copied[head % 2], 8 * b + head // 2)
                pe.wait_ge(probs_ready, H * b + head + 1)
                for c in range(CHUNKS):
                    mm = pe.transpose(probT_bank[head % 2][0:CK, c * T:(c + 1) * T],
                                      probs[head % 4][:, c * CK:(c + 1) * CK], ident[0:T, 0:T])
                mm.then_inc(probsT_ready, 1)

            def values(st, lag, quad):
                b, par = st.batch(lag), st.parity(lag)
                if quad == 0:
                    pe.wait_ge(proj_copied[0], 4 * b + 4)
                    pe.wait_ge(proj_copied[1], 4 * b + 4)
                    wait_count(pe, out_copied, b)
                pe.wait_ge(probsT_copied[0], 8 * b + 2 * quad + 2)
                pe.wait_ge(probsT_copied[1], 8 * b + 2 * quad + 2)
                for c in range(CHUNKS):
                    for r in range(4):
                        head = 4 * quad + r
                        mm = pe.matmul(out_bank[32 * r:32 * r + VW, quad * T:(quad + 1) * T],
                                       v_aug[par][:, c, head, :], probsT[head % 8][:, c, :],
                                       start=c == 0, stop=c == CHUNKS - 1)
                mm.then_inc(pv_done, 1)

            def transpose_context(b, par, half, j):
                pe.wait_ge(ctx_loaded[par], 16 * (half + 1))
                wait_count(pe, proj_copied[j], 4 * b)
                for c in range(CHUNKS):
                    mm = pe.transpose(proj_bank[j][:, c * CK:(c + 1) * CK],
                                      ctx_in[par][:, c, j * P:(j + 1) * P], ident[0:CK, 0:CK])
                mm.then_inc(proj_ready, 1)

            def projections(st, slot):
                b, par = st.batch(-1), st.parity(-1)
                if slot in (0, 3):
                    j = slot // 3
                    pe.wait_ge(proj_copied[0], 4 * b + 1)
                    pe.wait_ge(proj_copied[1], 4 * b + 1)
                    for k in range(DT):
                        for n, (w_part, c_part) in enumerate(PASSES):
                            mm = pe.matmul(proj_bank[j][:, 0:S], wk_parts[:, w_part, k, j * P:(j + 1) * P],
                                           ctx_parts[par][:, c_part, k, :], start=k == 0 and n == 0,
                                           stop=k == DT - 1 and n == len(PASSES) - 1)
                    mm.then_inc(proj_ready, 1)
                if slot in VALUES_SLOTS:
                    c = VALUES_SLOTS.index(slot)
                    if c % 2 == 0:
                        pe.wait_ge(proj_copied[c // 2], 4 * b + 3)
                    for k in range(DT):
                        for n, (w_part, c_part) in enumerate(PASSES):
                            mm = pe.matmul(proj_bank[c // 2][0:CK, (c % 2) * D:(c % 2 + 1) * D],
                                           ctx_parts[par][:, c_part, k, c * CK:(c + 1) * CK], wv_parts[:, w_part, k, :],
                                           start=k == 0 and n == 0, stop=k == DT - 1 and n == len(PASSES) - 1)
                    if c > 0:
                        mm.then_inc(proj_ready, 1)
                if slot == 4:
                    pe.wait_ge(proj_copied[0], 4 * b + 2)
                    pe.wait_ge(xn_ready, b + 1)
                    for j in range(DT):
                        mm = pe.transpose(proj_bank[0][:, j * T:(j + 1) * T], xn[:, j * P:(j + 1) * P], ident[0:T, 0:T])
                    mm.then_inc(proj_ready, 1)
                if slot == 6:
                    pe.wait_ge(proj_copied[1], 4 * b + 2)
                    pe.wait_ge(proj_copied[0], 4 * b + 3)
                    for j in range(DT):
                        for k in range(DT):
                            mm = pe.matmul(proj_bank[1][:, j * T:(j + 1) * T], wq_sb[:, k, j * P:(j + 1) * P],
                                           xnT[:, k, :], start=k == 0, stop=k == DT - 1)
                    mm.then_inc(proj_ready, 1)

            def tail(st, slot):
                if st.exists(2) and slot in (5, 8):
                    b = st.batch(2)
                    if slot == 5:
                        pe.wait_ge(tail_copied, 5 * b + 3)
                        pe.wait_ge(xr_ready, 2 * b + 1)
                        for j in range(DT):
                            mm = pe.transpose(tail_bank[:, j * T:(j + 1) * T], xr_now[:, j * P:(j + 1) * P],
                                              ident[0:T, 0:T])
                        mm.then_inc(tail_ready, 1)
                    else:
                        pe.wait_ge(tail_copied, 5 * b + 4)
                        for j in range(DT):
                            mm = pe.matmul(tail_bank[0:T, 0:EXPERTS], xrT[:, j, :], gw_sb[:, j, :],
                                           start=j == 0, stop=j == DT - 1)
                        mm.then_inc(tail_ready, 1)
                if st.exists(1) and slot in (10, 12, 14):
                    b = st.batch(1)
                    if slot == 10:
                        wait_count(pe, tail_copied, 5 * b)
                        pe.wait_ge(out_copied, b + 1)
                        for g in range(4):
                            mm = pe.transpose(tail_bank[0:T, g * P:(g + 1) * P], oT[:, g, :], ident[:, :])
                        mm.then_inc(tail_ready, 1)
                    elif slot == 12:
                        pe.wait_ge(tail_copied, 5 * b + 1)
                        for j in range(DT):
                            mm = pe.transpose(tail_bank[:, j * T:(j + 1) * T], att[:, j * P:(j + 1) * P], ident[0:T, 0:T])
                        mm.then_inc(tail_ready, 1)
                    else:
                        pe.wait_ge(tail_copied, 5 * b + 2)
                        for j in range(DT):
                            mm = pe.matmul(tail_bank[0:T, 0:D], attT[:, j, :], wo_sb[:, j, :],
                                           start=j == 0, stop=j == DT - 1)
                        mm.then_inc(tail_ready, 1)

            def step(st):
                for slot in range(H):
                    if st.exists(0):
                        scores(st, slot)
                    lag, head = (0, slot - HEAD_LAG_T) if slot >= HEAD_LAG_T else (1, H + slot - HEAD_LAG_T)
                    if st.exists(lag):
                        transpose_probs(st, lag, head)
                    if slot % 4 == 1:
                        lag, quad = (0, (slot - 9) // 4) if slot >= 9 else (1, 2 + slot // 4)
                        if st.exists(lag):
                            values(st, lag, quad)
                    if st.exists(-1):
                        projections(st, slot)
                    if st.exists(-2) and slot in CONTEXT_SLOTS:
                        transpose_context(st.batch(-2), st.parity(-2), st.half(-2), CONTEXT_SLOTS.index(slot))
                    tail(st, slot)

            for j in range(DT):
                transpose_context(0, 0, 0, j)
            run_steps(pe, step)

            pe.wait_ge(route_iota, 7)
            pe.wait_ge(route, R_ONEHOT)
            pe.matmul(ps[0:T, 0, 0:B * EXPERTS], upper[0:T, 0:T], small[3][0:T].rearrange("p b e -> p (b e)"),
                      start=True, stop=True).then_inc(ranks_ready, 1)
            pe.matmul(ps[:, 1, 0:B * EXPERTS], ones[0:T, :], small[3][0:T].rearrange("p b e -> p (b e)"),
                      start=True, stop=True).then_inc(ranks_ready, 1)

            def expert_of(t):
                return pe.value_load(tile_expert[0:1, bass.ds(t, 1)], min_val=0, max_val=EXPERTS - 1)

            def transpose_rows(t, buffer, nth, first):
                pe.wait_ge(xs_loaded[buffer], 16 * (nth + 1))
                if not first:
                    pe.wait_ge(x_low_ready, t)
                for j in range(DT):
                    mm = pe.transpose(ps[:, 0, j * P:(j + 1) * P], xs[buffer][:, j * P:(j + 1) * P], ident[:, :])
                mm.then_inc(xsT_ready, 1)

            def hidden(t, e, parity, first):
                pe.wait_ge(x_low_ready, t + 1)
                if not first:
                    pe.wait_ge(h_activated, 2 * t - 2)
                for f in range(FT):
                    for k in range(DT):
                        for n, (w_part, x_part) in enumerate(PASSES):
                            mm = pe.matmul(ps[:, 1 + 2 * parity + f // 4, (f % 4) * P:(f % 4 + 1) * P],
                                           w1_parts[:, w_part, bass.ds(e, 1), k, f * P:(f + 1) * P
                                                    ].rearrange("p o f -> p (o f)"),
                                           x_parts[parity][:, x_part, k, :], start=k == 0 and n == 0,
                                           stop=k == DT - 1 and n == len(PASSES) - 1)
                    if f % 4 == 3:
                        mm.then_inc(h_ready, 1)

            def outputs(t, e, parity, first):
                if not first:
                    pe.wait_ge(y_biased, t - 1)
                for f in range(FT):
                    if f % 4 == 0:
                        pe.wait_ge(h_low_ready, 2 * t + 1 + f // 4)
                    for n, (w_part, h_part) in enumerate(PASSES):
                        mm = pe.matmul(ps[:, 5 + parity, 0:D], h_parts[parity][:, h_part, f, :],
                                       w2_parts[:, w_part, bass.ds(e, 1), f, :].rearrange("p o d -> p (o d)"),
                                       start=f == 0 and n == 0, stop=f == FT - 1 and n == len(PASSES) - 1)
                mm.then_inc(y_ready, 1)

            pe.wait_ge(route, N_ROUTE)
            pe.wait_ge(w1_split, B)
            transpose_rows(0, 0, 0, True)
            transpose_rows(1, 1, 0, False)
            hidden(0, expert_of(0), 0, True)
            transpose_rows(2, 2, 0, False)
            hidden(1, expert_of(1), 1, True)
            pe.wait_ge(w2_loaded, 16 * EXPERTS)
            outputs(0, expert_of(0), 0, True)
            transpose_rows(3, 3, 0, False)
            hidden(2, expert_of(2), 0, False)
            outputs(1, expert_of(1), 1, True)
            with pe.Fori(0, FFN_LOOPS) as i:
                last_expert = expert_of(FFN_UNROLL * i + FFN_PEELED - 1)
                for k in range(FFN_UNROLL):
                    t = FFN_UNROLL * i + FFN_PEELED + k
                    transpose_rows(t + 1, k, i + 1, False)
                    expert = expert_of(t)
                    hidden(t, expert, (1 + k) % 2, False)
                    outputs(t - 1, last_expert, k % 2, False)
                    last_expert = expert
            for t in range(FFN_PEELED + FFN_UNROLL * FFN_LOOPS, FFN_TILES):
                if t + 1 < FFN_TILES:
                    transpose_rows(t + 1, (t + 1) % FFN_UNROLL, (t + 1) // FFN_UNROLL, False)
                hidden(t, expert_of(t), t % 2, False)
                outputs(t - 1, expert_of(t - 1), (t - 1) % 2, False)
            outputs(t, expert_of(t), t % 2, False)

        @block.vector
        def _(dve):
            dve.memset(v_aug[0], 1.0).then_inc(const_dve, 1)
            dve.memset(v_aug[1], 1.0).then_inc(const_dve, 1)
            dve.memset(out_bank, 0.0).then_inc(const_dve, 1)
            dve.memset(eps_ln, LN_EPS).then_inc(const_dve, 1)
            dve.memset(eps_rms, RMS_EPS).then_inc(const_dve, 1)
            dve.memset(minus_half, -0.5).then_inc(const_dve, 1)
            dve.memset(w_scale, SCALE_W).then_inc(const_dve, 1)
            dve.wait_ge(weights_loaded, 16 * N_WEIGHTS)
            nc.vector.tensor_copy(bv_rep, bv_cols.unsqueeze(2).to_broadcast([P, DT, T])).then_inc(const_dve, 1)
            def with_pairs_together(loaded):
                return loaded.rearrange("p t (j r i) -> p (t j) i r", i=32, r=PAIRS)

            def channels(weights):
                return weights.rearrange("p t (j i r) -> p (t j) i r", i=32, r=PAIRS)

            nc.vector.tensor_scalar(channels(wq_sb), with_pairs_together(wq_in), SCALE_Q * DH ** -0.5, None, ALU.mult
                                    ).then_inc(const_dve, 1)
            nc.vector.tensor_scalar(channels(wk_parts[:, 0]), with_pairs_together(wk_in), SCALE_K, None, ALU.mult
                                    ).then_inc(weights_high_ready, 1)
            nc.vector.tensor_scalar(wv_parts[:, 0], wv_in, SCALE_V, None, ALU.mult).then_inc(weights_high_ready, 1)
            dve.wait_ge(weights_high_ready, 2)
            for tj in range(DT * DT):
                nc.vector.scalar_tensor_tensor(
                    out=channels(wk_parts[:, 1])[:, tj], in0=with_pairs_together(wk_in)[:, tj], scalar=SCALE_K,
                    in1=channels(wk_parts[:, 0])[:, tj], op0=ALU.mult, op1=ALU.subtract).then_inc(const_dve, 1)
            nc.vector.scalar_tensor_tensor(out=wv_parts[:, 1], in0=wv_in, scalar=SCALE_V, in1=wv_parts[:, 0],
                                           op0=ALU.mult, op1=ALU.subtract).then_inc(const_dve, 1)
            for bias, scale in ((bk_sb, SCALE_K), (bq_sb, SCALE_Q * DH ** -0.5)):
                nc.vector.tensor_scalar(bias, bias, scale, None, ALU.mult).then_inc(const_dve, 1)
            dve.wait_ge(constants, N_CONST_POOL)
            nc.vector.tensor_reduce(pair_rows, ident[:, :].rearrange("p (a i) -> p a i", a=2),
                                    AX_X, ALU.add).then_inc(const_dve, 1)
            nc.vector.tensor_scalar(mask_bias, mask_bias, NEG_BIG, SCALE_SCORES, ALU.mult, ALU.mult
                                    ).then_inc(mask_ready, 1)
            dve.wait_ge(setup_pe, 2)
            nc.vector.tensor_tensor(bvo, proj_bank[0][0:T, 0:D], bvo, ALU.add).then_inc(setup_copied, 1)
            dve.wait_ge(mask_ready, 1)

            def context_low(b, par, j):
                dve.wait_ge(ctx_high_ready, DT * b + j + 1)
                nc.vector.tensor_tensor(ctx_parts[par][:, 1, j, :], proj_bank[j][:, 0:S], ctx_parts[par][:, 0, j, :],
                                        ALU.subtract).then_inc(proj_copied[j], 1)

            def queries_stats(b, parity, half):
                dve.wait_ge(x_loaded[parity], 16 * (half + 1))
                nc.vector.bn_stats(st1, x_in[parity]).then_inc(ln1_stats, 1)
                wait_apart(dve, ln1_stats, b + 1, dve_passed)
                nc.vector.bn_aggr(mv1, st1).then_inc(ln1_mean, 1)

            def step(st):
                for slot in range(H):
                    lag, head = (0, slot - HEAD_LAG_COPY) if slot >= HEAD_LAG_COPY else (1, H + slot - HEAD_LAG_COPY)
                    if head % 2 == 1 and st.exists(lag):
                        dve.wait_ge(probsT_ready, H * st.batch(lag) + head + 1)
                        wait_count(dve, pv_done, 4 * st.batch(lag) + head // 4 - 1)
                        nc.vector.tensor_copy(probsT[head % 8], probT_bank[head % 2][0:CK, 0:CHUNKS * T].rearrange(
                            "p (c t) -> p c t", c=CHUNKS)).then_inc(probsT_copied[1], 1)
                    if st.exists(-1):
                        b, par = st.batch(-1), st.parity(-1)
                        if slot in (2, 5):
                            j = slot // 5
                            dve.wait_ge(k_high_ready, DT * b + j + 1)
                            nc.vector.scalar_tensor_tensor(
                                out=k_parts[:, 1, j, :], in0=proj_bank[j][:, 0:S], scalar=bk_sb[:, j:j + 1],
                                in1=k_parts[:, 0, j, :], op0=ALU.add, op1=ALU.subtract).then_inc(proj_copied[j], 1)
                        if slot == 7:
                            dve.wait_ge(proj_ready, 8 * b + 6)
                            wait_count(dve, q_parts_ready, b)
                            for j, done in ((0, q1_ready), (1, proj_copied[1])):
                                nc.vector.tensor_scalar(q1[:, j, :], proj_bank[1][:, j * T:(j + 1) * T],
                                                        bq_sb[:, j:j + 1], None, ALU.add
                                                        ).then_inc(done, 1)
                    if st.exists(-2) and slot - 2 in CONTEXT_SLOTS:
                        context_low(st.batch(-2), st.parity(-2), CONTEXT_SLOTS.index(slot - 2))
                    if st.exists(-2) and slot == 10:
                        queries_stats(st.batch(-2), st.parity(-2), st.half(-2))
                    if st.exists(2) and slot == 9:
                        b = st.batch(2)
                        dve.wait_ge(tail_ready, 5 * b + 5)
                        nc.vector.tensor_copy(gate_logits[:, bass.ds(b, 1), :].rearrange("p o e -> p (o e)"),
                                              tail_bank[0:T, 0:EXPERTS]).then_inc(tail_copied, 1)
                    if st.exists(1):
                        b, par = st.batch(1), st.parity(1)
                        if slot == 11:
                            heads = tail_bank[0:T, :].rearrange("p (h w) -> p h w", w=32)
                            dve.wait_ge(tail_ready, 5 * b + 1)
                            nc.vector.reciprocal(rden, heads[:, :, DH]).then_inc(rden_ready, 1)
                            dve.wait_ge(rden_ready, b + 1)
                            nc.vector.tensor_tensor(att.rearrange("p (h d) -> p h d", h=H), heads[:, :, 0:DH],
                                                    rden.unsqueeze(2).to_broadcast([T, H, DH]), ALU.mult
                                                    ).then_inc(tail_copied, 1)
                    if st.exists(2) and slot == 4:
                        b, par = st.batch(2), st.parity(2)
                        wait_count(dve, xr_ready, 2 * b)
                        dve.wait_ge(ln2_chain, 7 * b + 7)
                        nc.vector.tensor_scalar(centred, x1[par], mv2[:, 0:1], ln2[:, 6:7], ALU.subtract,
                                                ALU.mult).then_inc(centred_ready, 1)
                    if st.exists(0):
                        b = st.batch(0)
                        wait_count(dve, probsT_ready, H * b + slot - 3)
                        wait_apart(dve, scores_ready, H * b + slot + 1, dve_passed)
                        nc.vector.tensor_tensor_reduce(
                            out=probs[slot % 4], in0=score_bank[slot % 2][0:T, 0:S], in1=mask_bias, scale=-1.0 / SCALE_SCORES,
                            scalar=3.4e38, op0=ALU.add, op1=ALU.min,
                            accum_out=minus_max[:, slot % 4:slot % 4 + 1]).then_inc(max_ready, 1)
                    if st.exists(-1):
                        b, par = st.batch(-1), st.parity(-1)
                        if slot == 1:
                            dve.wait_ge(rstd_ready, b + 1)
                            nc.vector.tensor_scalar(xn, x_in[par], mv1[:, 0:1], rstd[:, 0:1], ALU.subtract,
                                                    ALU.mult).then_inc(xn_ready, 1)
                    if st.exists(1):
                        b, par = st.batch(1), st.parity(1)
                        if slot == 15:
                            dve.wait_ge(tail_ready, 5 * b + 3)
                            dve.wait_ge(res_ready, b + 1)
                            wait_count(dve, x1_spilled[par], 16 * st.half(1))
                            nc.vector.tensor_tensor(x1[par], tail_bank[0:T, 0:D], x_res[par], ALU.add
                                                    ).then_inc(tail_copied, 1)
                            dve.wait_ge(tail_copied, 5 * b + 3)
                            nc.vector.bn_stats(st2, x1[par]).then_inc(ln2_stats, 1)
                            wait_apart(dve, ln2_stats, b + 1, dve_passed)
                            nc.vector.bn_aggr(mv2, st2).then_inc(ln2_mean, 1)

            for j in range(DT):
                context_low(0, 0, j)
            queries_stats(0, 0, 0)
            run_steps(dve, step)

            done = [0]

            def link(instruction):
                done[0] += 1
                instruction.then_inc(route, 1)
                dve.wait_ge(route, done[0])

            def over_experts(ap):
                return ap.unsqueeze(2).to_broadcast([T, B, EXPERTS])

            order, diff, exps, onehot, weighted, rank, counts, scan_a, scan_b = [s for s in small]
            gmax, gsum, emax, wmax, slot_f = [small_b[0:T, i, :] for i in range(5)]
            dve.wait_ge(tail_copied, 5 * B)
            link(nc.vector.tensor_reduce(gmax, gate_logits[:, :, :], AX_X, ALU.max))
            link(nc.vector.tensor_tensor(diff[0:T], gate_logits[:, :, :], over_experts(gmax), ALU.subtract))
            assert done[0] == R_DIFF
            dve.wait_ge(route_exp, 1)
            link(nc.vector.tensor_reduce(gsum, exps[0:T], AX_X, ALU.add))
            link(nc.vector.tensor_reduce(emax, exps[0:T], AX_X, ALU.max))
            link(nc.vector.reciprocal(wmax, gsum))
            link(nc.vector.tensor_tensor(xr_all[:, :, D], emax, wmax, ALU.mult))
            link(nc.vector.tensor_tensor(weighted[0:T], exps[0:T], over_experts(emax), ALU.is_equal))
            dve.wait_ge(route_iota, 2)
            link(nc.vector.tensor_tensor(weighted[0:T], weighted[0:T], order[0:T], ALU.mult))
            link(nc.vector.tensor_reduce(wmax, weighted[0:T], AX_X, ALU.max))
            link(nc.vector.tensor_tensor(onehot[0:T], weighted[0:T], over_experts(wmax), ALU.is_equal))
            assert done[0] == R_ONEHOT
            dve.wait_ge(ranks_ready, 2)
            link(nc.vector.tensor_copy(rank[0:T], ps[0:T, 0, 0:B * EXPERTS].rearrange("p (b e) -> p b e", b=B)))
            link(nc.vector.tensor_copy(counts, ps[:, 1, 0:B * EXPERTS].rearrange("p (b e) -> p b e", b=B)))
            link(nc.vector.tensor_copy(scan_a, counts))
            a, c = scan_a, scan_b
            for k in (1, 2, 4, 8, 16):
                nc.vector.tensor_copy(c[:, 0:k, :], a[:, 0:k, :])
                link(nc.vector.tensor_tensor(c[:, k:B, :], a[:, k:B, :], a[:, 0:B - k, :], ALU.add))
                a, c = c, a
            total = a[:, B - 1, :]
            dve.wait_ge(route_iota, 11)
            tiles_e, cum0, cum1, start = [small_e[:, i, :] for i in range(4)]
            link(nc.vector.tensor_tensor(small_te, small_te, total.unsqueeze(2).to_broadcast([P, EXPERTS, B]),
                                         ALU.is_lt))
            link(nc.vector.tensor_reduce(tiles_e, small_te, AX_X, ALU.add))
            link(nc.vector.tensor_copy(cum0, tiles_e))
            u, v = cum0, cum1
            for k in (1, 2, 4):
                nc.vector.tensor_copy(v[:, 0:k], u[:, 0:k])
                link(nc.vector.tensor_tensor(v[:, k:EXPERTS], u[:, k:EXPERTS], u[:, 0:EXPERTS - k], ALU.add))
                u, v = v, u
            link(nc.vector.tensor_tensor(start, u, tiles_e, ALU.subtract))
            link(nc.vector.tensor_scalar(start, start, float(P), None, ALU.mult))
            link(nc.vector.tensor_tensor(rank[0:T], rank[0:T], a[0:T], ALU.add))
            link(nc.vector.tensor_tensor(rank[0:T], rank[0:T], counts[0:T], ALU.subtract))
            link(nc.vector.tensor_tensor(rank[0:T], rank[0:T],
                                         start[0:T].unsqueeze(1).to_broadcast([T, B, EXPERTS]), ALU.add))
            link(nc.vector.tensor_tensor(rank[0:T], rank[0:T], onehot[0:T], ALU.mult))
            link(nc.vector.tensor_reduce(slot_f, rank[0:T], AX_X, ALU.add))
            link(nc.vector.tensor_copy(slot_of[:, :], slot_f))
            link(nc.vector.tensor_tensor(tile_cmp, tile_no, u[0:1].unsqueeze(1).to_broadcast([1, FFN_TILES, EXPERTS]),
                                         ALU.is_ge))
            link(nc.vector.tensor_reduce(tile_sum, tile_cmp, AX_X, ALU.add))
            link(nc.vector.tensor_scalar(tile_expert[:, 0:FFN_TILES], tile_sum, float(EXPERTS - 1), None, ALU.min))
            assert done[0] == N_ROUTE, done

            def number_tokens(t, buffer, nth, first):
                dve.wait_ge(xs_loaded[buffer], 16 * (nth + 1))
                if not first:
                    dve.wait_ge(out_stored[buffer], 16 * nth)
                nc.vector.tensor_scalar(token_of[buffer], xs[buffer][:, D + 1:D + 2], -1.0, float(NO_TOKEN),
                                        ALU.mult, ALU.add).then_inc(token_ready, 1)

            def rows_low(t, parity):
                dve.wait_ge(x_high_ready, t + 1)
                nc.vector.scalar_tensor_tensor(
                    out=x_parts[parity][:, 1], in0=ps[:, 0, 0:DT * P].rearrange("p (j t) -> p j t", j=DT),
                    scalar=SCALE_X, in1=x_parts[parity][:, 0], op0=ALU.mult, op1=ALU.subtract
                    ).then_inc(x_low_ready, 1)

            def split_hidden(t, parity, first):
                if not first:
                    dve.wait_ge(y_ready, t - 1)
                for half in range(2):
                    f = slice(FT // 2 * half, FT // 2 * (half + 1))
                    dve.wait_ge(h_activated, 2 * t + 1 + half)
                    nc.vector.tensor_scalar(h_parts[parity][:, 0, f], h_act[:, f], SCALE_X, None, ALU.mult
                                            ).then_inc(h_high_ready, 1)
                    dve.wait_ge(h_high_ready, 2 * t + 1 + half)
                    nc.vector.scalar_tensor_tensor(
                        out=h_parts[parity][:, 1, f], in0=h_act[:, f], scalar=SCALE_X, in1=h_parts[parity][:, 0, f],
                        op0=ALU.mult, op1=ALU.subtract).then_inc(h_low_ready, 1)

            def add_y(t, buffer, half, nth):
                parity = buffer % 2
                dve.wait_ge(b2_loaded[parity], 16 * (half + 1))
                wait_count(dve, out_ready, t)
                dve.wait_ge(y_ready, t + 1)
                nc.vector.scalar_tensor_tensor(out=y_sb, in0=ps[:, 5 + parity, 0:D],
                                               scalar=1.0 / (SCALE_W * SCALE_X), in1=b2_rep[parity], op0=ALU.mult,
                                               op1=ALU.add).then_inc(y_biased, 1)
                dve.wait_ge(y_biased, t + 1)
                dve.wait_ge(x1_gathered[buffer], 16 * (nth + 1))
                nc.vector.scalar_tensor_tensor(out=out_rows[buffer], in0=y_sb, scalar=xs[buffer][:, D:D + 1],
                                               in1=x1_got[buffer], op0=ALU.mult, op1=ALU.add).then_inc(out_ready, 1)

            dve.wait_ge(scattered, 16 * B)
            number_tokens(0, 0, 0, True)
            rows_low(0, 0)
            number_tokens(1, 1, 0, True)
            rows_low(1, 1)
            split_hidden(0, 0, True)
            number_tokens(2, 2, 0, True)
            rows_low(2, 0)
            split_hidden(1, 1, True)
            add_y(0, 0, 0, 0)
            number_tokens(3, 3, 0, True)
            rows_low(3, 1)
            split_hidden(2, 0, False)
            add_y(1, 1, 0, 0)
            with dve.Fori(0, FFN_LOOPS) as i:
                for k in range(FFN_UNROLL):
                    t = FFN_UNROLL * i + FFN_PEELED + k
                    number_tokens(t + 1, k, i + 1, False)
                    rows_low(t + 1, k % 2)
                    split_hidden(t, (1 + k) % 2, False)
                    buffer = (k + 2) % FFN_UNROLL
                    add_y(t - 1, buffer, 2 * i + (k + 2) // 2, i + (k + 2) // FFN_UNROLL)
            for t in range(FFN_PEELED + FFN_UNROLL * FFN_LOOPS, FFN_TILES):
                if t + 1 < FFN_TILES:
                    number_tokens(t + 1, (t + 1) % FFN_UNROLL, (t + 1) // FFN_UNROLL, False)
                    rows_low(t + 1, (t + 1) % 2)
                split_hidden(t, t % 2, False)
                add_y(t - 1, (t - 1) % FFN_UNROLL, (t - 1) // 2, (t - 1) // FFN_UNROLL)
            add_y(t, t % FFN_UNROLL, t // 2, t // FFN_UNROLL)


R_DIFF, R_ONEHOT, N_ROUTE = 2, 10, 35

_INS = ["x", "ctx_1024", "mask_1x1xSxS2_fk1", "L0_xattn_wq_w", "L0_xattn_wq_b", "L0_xattn_wk_w", "L0_xattn_wk_b",
        "L0_xattn_wv_w", "L0_xattn_wv_b", "L0_xattn_wo_w", "L0_xattn_wo_b", "L0_ffn_rms_w", "L0_ffn_gate_w",
        "L0_ffn_W1", "L0_ffn_b1", "L0_ffn_W2", "L0_ffn_b2"]


def kernel(**inputs):
    import numpy as np
    import concourse.bacc as bacc
    from concourse.bass_utils import run_bass_kernel_spmd

    nc = bacc.Bacc("TRN2", target_bir_lowering=False, num_devices=1)
    arrays, args = {}, []
    for name in _INS:
        a = np.ascontiguousarray(inputs[name])
        arrays[f"in_{name}"] = a
        args.append(nc.dram_tensor(f"in_{name}", a.shape, mybir.dt.from_np(a.dtype), kind="ExternalInput").ap())
    out = nc.dram_tensor("out", (B, T, D), F32, kind="ExternalOutput").ap()
    build(nc, *args, out)
    r = run_bass_kernel_spmd(nc, [arrays], core_ids=[0])
    return r.results[0]["out"]
```
